# Optimizing a Trainium2 kernel written in Bass

```python
import numpy as np
import jax
import jax.numpy as jnp

def _softmax(x, axis=-1):
    return jax.nn.softmax(x, axis=axis)

def _gelu(x):
    return jax.nn.gelu(x, approximate=True)

def _silu(x):
    return jax.nn.silu(x)

def _sigmoid(x):
    return jax.nn.sigmoid(x)

def _layernorm(x, axis=-1, eps=1e-05):
    m = jnp.mean(x, axis=axis, keepdims=True)
    v = jnp.var(x, axis=axis, keepdims=True)
    return (x - m) / jnp.sqrt(v + eps)

def _scatter_add(tgt, idx, src, axis=0):
    return tgt.at[idx].add(src)

def _segment_sum(src, seg, n):
    return jax.ops.segment_sum(src, seg, n)
kernel_name = 'mk_rec_standalone_d1_rec_r8_0d486d'

def setup_inputs(seed: int=0):
    np.random.seed(seed)
    _w = jnp.asarray

    def _rec_inputs():
        import jax
        import jax.numpy as jnp
        _rk = jax.random.key(seed)
        r_cont_features = -0.0020667 + 0.996956 * jax.random.normal(jax.random.fold_in(_rk, 1), (1024, 20), jnp.float32)
        r_item_id = jax.random.randint(jax.random.fold_in(_rk, 2), (1024,), 72, 499898, jnp.int32)
        r_past_interactions = jnp.stack([jax.random.randint(jax.random.fold_in(jax.random.fold_in(_rk, 3), 0), (1024,), 4, 499959, jnp.int32), jax.random.randint(jax.random.fold_in(jax.random.fold_in(_rk, 3), 1), (1024,), 13, 499973, jnp.int32), jax.random.randint(jax.random.fold_in(jax.random.fold_in(_rk, 3), 2), (1024,), 26, 62495, jnp.int32), jax.random.randint(jax.random.fold_in(jax.random.fold_in(_rk, 3), 3), (1024,), 49, 499859, jnp.int32), jax.random.randint(jax.random.fold_in(jax.random.fold_in(_rk, 3), 4), (1024,), 23, 499998, jnp.int32), jax.random.randint(jax.random.fold_in(jax.random.fold_in(_rk, 3), 5), (1024,), 54, 499981, jnp.int32), jax.random.randint(jax.random.fold_in(jax.random.fold_in(_rk, 3), 6), (1024,), 107, 499998, jnp.int32), jax.random.randint(jax.random.fold_in(jax.random.fold_in(_rk, 3), 7), (1024,), 20, 499983, jnp.int32), jax.random.randint(jax.random.fold_in(jax.random.fold_in(_rk, 3), 8), (1024,), 37, 499994, jnp.int32), jax.random.randint(jax.random.fold_in(jax.random.fold_in(_rk, 3), 9), (1024,), 110, 499978, jnp.int32)], axis=1)
        r_price_rank = jax.random.randint(jax.random.fold_in(_rk, 4), (1024,), 0, 30, jnp.int32)
        r_city = jax.random.randint(jax.random.fold_in(_rk, 5), (1024,), 4, 49998, jnp.int32)
        r_last_item = jax.random.randint(jax.random.fold_in(_rk, 6), (1024,), 23, 499991, jnp.int32)
        r_impression_index = jax.random.randint(jax.random.fold_in(_rk, 7), (1024,), 0, 30, jnp.int32)
        r_past_interactions_sess = jnp.stack([jax.random.randint(jax.random.fold_in(jax.random.fold_in(_rk, 8), 0), (1024,), 49, 499965, jnp.int32), jax.random.randint(jax.random.fold_in(jax.random.fold_in(_rk, 8), 1), (1024,), 161, 499948, jnp.int32), jax.random.randint(jax.random.fold_in(jax.random.fold_in(_rk, 8), 2), (1024,), 106, 499879, jnp.int32), jax.random.randint(jax.random.fold_in(jax.random.fold_in(_rk, 8), 3), (1024,), 67, 62497, jnp.int32), jax.random.randint(jax.random.fold_in(jax.random.fold_in(_rk, 8), 4), (1024,), 14, 499931, jnp.int32), jax.random.randint(jax.random.fold_in(jax.random.fold_in(_rk, 8), 5), (1024,), 28, 499850, jnp.int32), jax.random.randint(jax.random.fold_in(jax.random.fold_in(_rk, 8), 6), (1024,), 85, 62492, jnp.int32), jax.random.randint(jax.random.fold_in(jax.random.fold_in(_rk, 8), 7), (1024,), 67, 499943, jnp.int32), jax.random.randint(jax.random.fold_in(jax.random.fold_in(_rk, 8), 8), (1024,), 75, 499978, jnp.int32), jax.random.randint(jax.random.fold_in(jax.random.fold_in(_rk, 8), 9), (1024,), 55, 62500, jnp.int32), jax.random.randint(jax.random.fold_in(jax.random.fold_in(_rk, 8), 10), (1024,), 5, 499957, jnp.int32), jax.random.randint(jax.random.fold_in(jax.random.fold_in(_rk, 8), 11), (1024,), 42, 62493, jnp.int32), jax.random.randint(jax.random.fold_in(jax.random.fold_in(_rk, 8), 12), (1024,), 58, 499853, jnp.int32), jax.random.randint(jax.random.fold_in(jax.random.fold_in(_rk, 8), 13), (1024,), 33, 499945, jnp.int32), jax.random.randint(jax.random.fold_in(jax.random.fold_in(_rk, 8), 14), (1024,), 55, 499990, jnp.int32), jax.random.randint(jax.random.fold_in(jax.random.fold_in(_rk, 8), 15), (1024,), 132, 499961, jnp.int32), jax.random.randint(jax.random.fold_in(jax.random.fold_in(_rk, 8), 16), (1024,), 60, 499988, jnp.int32), jax.random.randint(jax.random.fold_in(jax.random.fold_in(_rk, 8), 17), (1024,), 2, 499987, jnp.int32), jax.random.randint(jax.random.fold_in(jax.random.fold_in(_rk, 8), 18), (1024,), 198, 499950, jnp.int32), jax.random.randint(jax.random.fold_in(jax.random.fold_in(_rk, 8), 19), (1024,), 46, 499940, jnp.int32), jax.random.randint(jax.random.fold_in(jax.random.fold_in(_rk, 8), 20), (1024,), 10, 499940, jnp.int32), jax.random.randint(jax.random.fold_in(jax.random.fold_in(_rk, 8), 21), (1024,), 20, 62495, jnp.int32), jax.random.randint(jax.random.fold_in(jax.random.fold_in(_rk, 8), 22), (1024,), 1, 499980, jnp.int32), jax.random.randint(jax.random.fold_in(jax.random.fold_in(_rk, 8), 23), (1024,), 111, 499972, jnp.int32), jax.random.randint(jax.random.fold_in(jax.random.fold_in(_rk, 8), 24), (1024,), 16, 499974, jnp.int32), jax.random.randint(jax.random.fold_in(jax.random.fold_in(_rk, 8), 25), (1024,), 42, 499951, jnp.int32), jax.random.randint(jax.random.fold_in(jax.random.fold_in(_rk, 8), 26), (1024,), 47, 499988, jnp.int32), jax.random.randint(jax.random.fold_in(jax.random.fold_in(_rk, 8), 27), (1024,), 129, 499972, jnp.int32), jax.random.randint(jax.random.fold_in(jax.random.fold_in(_rk, 8), 28), (1024,), 7, 499957, jnp.int32), jax.random.randint(jax.random.fold_in(jax.random.fold_in(_rk, 8), 29), (1024,), 91, 62500, jnp.int32)], axis=1)
        r_past_actions_sess = jax.random.randint(jax.random.fold_in(_rk, 9), (1024, 30), 0, 10, jnp.int32)
        r_last_click_item = jax.random.randint(jax.random.fold_in(_rk, 10), (1024,), 24, 499985, jnp.int32)
        r_last_click_impression = jax.random.randint(jax.random.fold_in(_rk, 11), (1024,), 0, 30, jnp.int32)
        r_last_interact_index = jax.random.randint(jax.random.fold_in(_rk, 12), (1024,), 0, 30, jnp.int32)
        r_neighbor_prices = 0.0013539 + 1.0001 * jax.random.normal(jax.random.fold_in(_rk, 13), (1024, 25), jnp.float32)
        r_city_platform = jax.random.randint(jax.random.fold_in(_rk, 14), (1024,), 3, 59994, jnp.int32)
        return (r_cont_features, r_item_id, r_past_interactions, r_price_rank, r_city, r_last_item, r_impression_index, r_past_interactions_sess, r_past_actions_sess, r_last_click_item, r_last_click_impression, r_last_interact_index, r_neighbor_prices, r_city_platform)
    r_cont_features, r_item_id, r_past_interactions, r_price_rank, r_city, r_last_item, r_impression_index, r_past_interactions_sess, r_past_actions_sess, r_last_click_item, r_last_click_impression, r_last_interact_index, r_neighbor_prices, r_city_platform = _rec_inputs()

    def _L0_rec_setup():
        import jax, jax.numpy as jnp
        import numpy as np
        EMB = 128
        H = 64
        EPS = 1e-05

        def _bn(x, g, b):
            m = jnp.mean(x, axis=0)
            v = jnp.var(x, axis=0)
            return (x - m) * jax.lax.rsqrt(v + EPS) * g + b

        def _gru_dir(x, wih, whh, bih, bhh):
            B = x.shape[0]
            pre = jnp.einsum('bti,gi->btg', x, wih) + bih

            def step(h, p):
                hr = h @ whh[:H].T + bhh[:H]
                hz = h @ whh[H:2 * H].T + bhh[H:2 * H]
                hn = h @ whh[2 * H:].T + bhh[2 * H:]
                r = jax.nn.sigmoid(p[:, :H] + hr)
                z = jax.nn.sigmoid(p[:, H:2 * H] + hz)
                n = jnp.tanh(p[:, 2 * H:] + r * hn)
                h = (1.0 - z) * n + z * h
                return (h, h)
            h0 = jnp.zeros((B, H), x.dtype)
            _, hs = jax.lax.scan(step, h0, jnp.swapaxes(pre, 0, 1))
            return jnp.swapaxes(hs, 0, 1)

        def _bigru_layer(x, wih, whh, bih, bhh):
            fwd = _gru_dir(x, wih[0], whh[0], bih[0], bhh[0])
            bwd = _gru_dir(x[:, ::-1], wih[1], whh[1], bih[1], bhh[1])[:, ::-1]
            return jnp.concatenate([fwd, bwd], axis=-1)
        key = jax.random.key(seed)
        ks = jax.random.split(key, 48)
        B = 1024
        V_ITEM, V_PRICE, V_CITY, V_IMP, V_ACT, V_CP = (62500, 30, 6250, 30, 10, 7500)
        f32 = jnp.float32
        inp = {'item_id': jax.random.randint(ks[0], (B,), 0, V_ITEM), 'past_interactions': jax.random.randint(ks[1], (B, 10), 0, V_ITEM), 'mask': jnp.ones((B, 10), dtype=bool), 'price_rank': jax.random.randint(ks[2], (B,), 0, V_PRICE), 'city': jax.random.randint(ks[3], (B,), 0, V_CITY), 'last_item': jax.random.randint(ks[4], (B,), 0, V_ITEM), 'impression_index': jax.random.randint(ks[5], (B,), 0, V_IMP), 'cont_features': jax.random.normal(ks[6], (B, 20), f32), 'past_interactions_sess': jax.random.randint(ks[7], (B, 30), 0, V_ITEM), 'past_actions_sess': jax.random.randint(ks[8], (B, 30), 0, V_ACT), 'last_click_item': jax.random.randint(ks[9], (B,), 0, V_ITEM), 'last_click_impression': jax.random.randint(ks[10], (B,), 0, V_IMP), 'last_interact_index': jax.random.randint(ks[11], (B,), 0, V_IMP), 'neighbor_prices': jax.random.normal(ks[12], (B, 25), f32), 'city_platform': jax.random.randint(ks[13], (B,), 0, V_CP)}
        inp['emb_item'] = jax.random.normal(ks[14], (V_ITEM, EMB), f32)
        inp['emb_price'] = jax.random.normal(ks[15], (V_PRICE, EMB), f32)
        inp['emb_city'] = jax.random.normal(ks[16], (V_CITY, EMB), f32)
        inp['emb_imp'] = jax.random.normal(ks[17], (V_IMP, EMB), f32)
        inp['emb_act'] = jax.random.normal(ks[18], (V_ACT, EMB), f32)
        inp['emb_cp'] = jax.random.normal(ks[19], (V_CP, EMB), f32)
        s = 0.1
        inp['gru_wih0'] = jax.random.normal(ks[20], (2, 3 * H, 2 * EMB), f32) * s
        inp['gru_whh0'] = jax.random.normal(ks[21], (2, 3 * H, H), f32) * s
        inp['gru_bih0'] = jax.random.normal(ks[22], (2, 3 * H), f32) * s
        inp['gru_bhh0'] = jax.random.normal(ks[23], (2, 3 * H), f32) * s
        inp['gru_wih1'] = jax.random.normal(ks[24], (2, 3 * H, 2 * H), f32) * s
        inp['gru_whh1'] = jax.random.normal(ks[25], (2, 3 * H, H), f32) * s
        inp['gru_bih1'] = jax.random.normal(ks[26], (2, 3 * H), f32) * s
        inp['gru_bhh1'] = jax.random.normal(ks[27], (2, 3 * H), f32) * s
        inp['bn_g'] = jnp.ones((1920,), f32)
        inp['bn_b'] = jnp.zeros((1920,), f32)
        inp['w1'] = jax.random.normal(ks[28], (1852, 1920), f32) * 0.02
        inp['b1'] = jnp.zeros((1852,), f32)
        inp['w2'] = jax.random.normal(ks[29], (256, 1920), f32) * 0.02
        inp['b2'] = jnp.zeros((256,), f32)
        inp['wout'] = jax.random.normal(ks[30], (256,), f32) * 0.02
        inp['bout'] = jnp.zeros((), f32)
        return inp
    _L0_rec_all = _L0_rec_setup()
    _L0_rec_in = {k: v for k, v in _L0_rec_all.items() if k in ('mask', 'emb_item', 'emb_price', 'emb_city', 'emb_imp', 'emb_act', 'emb_cp', 'gru_wih0', 'gru_whh0', 'gru_bih0', 'gru_bhh0', 'gru_wih1', 'gru_whh1', 'gru_bih1', 'gru_bhh1', 'bn_g', 'bn_b', 'w1', 'b1', 'w2', 'b2', 'wout', 'bout')}
    del _L0_rec_all
    return {'r_cont_features': r_cont_features, 'r_item_id': r_item_id, 'r_past_interactions': r_past_interactions, 'r_price_rank': r_price_rank, 'r_city': r_city, 'r_last_item': r_last_item, 'r_impression_index': r_impression_index, 'r_past_interactions_sess': r_past_interactions_sess, 'r_past_actions_sess': r_past_actions_sess, 'r_last_click_item': r_last_click_item, 'r_last_click_impression': r_last_click_impression, 'r_last_interact_index': r_last_interact_index, 'r_neighbor_prices': r_neighbor_prices, 'r_city_platform': r_city_platform, 'L0_rec_mask': _L0_rec_in['mask'], 'L0_rec_emb_item': _L0_rec_in['emb_item'], 'L0_rec_emb_price': _L0_rec_in['emb_price'], 'L0_rec_emb_city': _L0_rec_in['emb_city'], 'L0_rec_emb_imp': _L0_rec_in['emb_imp'], 'L0_rec_emb_act': _L0_rec_in['emb_act'], 'L0_rec_emb_cp': _L0_rec_in['emb_cp'], 'L0_rec_gru_wih0': _L0_rec_in['gru_wih0'], 'L0_rec_gru_whh0': _L0_rec_in['gru_whh0'], 'L0_rec_gru_bih0': _L0_rec_in['gru_bih0'], 'L0_rec_gru_bhh0': _L0_rec_in['gru_bhh0'], 'L0_rec_gru_wih1': _L0_rec_in['gru_wih1'], 'L0_rec_gru_whh1': _L0_rec_in['gru_whh1'], 'L0_rec_gru_bih1': _L0_rec_in['gru_bih1'], 'L0_rec_gru_bhh1': _L0_rec_in['gru_bhh1'], 'L0_rec_bn_g': _L0_rec_in['bn_g'], 'L0_rec_bn_b': _L0_rec_in['bn_b'], 'L0_rec_w1': _L0_rec_in['w1'], 'L0_rec_b1': _L0_rec_in['b1'], 'L0_rec_w2': _L0_rec_in['w2'], 'L0_rec_b2': _L0_rec_in['b2'], 'L0_rec_wout': _L0_rec_in['wout'], 'L0_rec_bout': _L0_rec_in['bout']}

def reference(r_cont_features, r_item_id, r_past_interactions, r_price_rank, r_city, r_last_item, r_impression_index, r_past_interactions_sess, r_past_actions_sess, r_last_click_item, r_last_click_impression, r_last_interact_index, r_neighbor_prices, r_city_platform, L0_rec_mask, L0_rec_emb_item, L0_rec_emb_price, L0_rec_emb_city, L0_rec_emb_imp, L0_rec_emb_act, L0_rec_emb_cp, L0_rec_gru_wih0, L0_rec_gru_whh0, L0_rec_gru_bih0, L0_rec_gru_bhh0, L0_rec_gru_wih1, L0_rec_gru_whh1, L0_rec_gru_bih1, L0_rec_gru_bhh1, L0_rec_bn_g, L0_rec_bn_b, L0_rec_w1, L0_rec_b1, L0_rec_w2, L0_rec_b2, L0_rec_wout, L0_rec_bout):
    import jax
    import jax.numpy as jnp

    def _L0_rec_ref(item_id, past_interactions, mask, price_rank, city, last_item, impression_index, cont_features, past_interactions_sess, past_actions_sess, last_click_item, last_click_impression, last_interact_index, neighbor_prices, city_platform, emb_item, emb_price, emb_city, emb_imp, emb_act, emb_cp, gru_wih0, gru_whh0, gru_bih0, gru_bhh0, gru_wih1, gru_whh1, gru_bih1, gru_bhh1, bn_g, bn_b, w1, b1, w2, b2, wout, bout):
        import jax, jax.numpy as jnp
        import numpy as np
        EMB = 128
        H = 64
        EPS = 1e-05

        def _bn(x, g, b):
            m = jnp.mean(x, axis=0)
            v = jnp.var(x, axis=0)
            return (x - m) * jax.lax.rsqrt(v + EPS) * g + b

        def _gru_dir(x, wih, whh, bih, bhh):
            B = x.shape[0]
            pre = jnp.einsum('bti,gi->btg', x, wih) + bih

            def step(h, p):
                hr = h @ whh[:H].T + bhh[:H]
                hz = h @ whh[H:2 * H].T + bhh[H:2 * H]
                hn = h @ whh[2 * H:].T + bhh[2 * H:]
                r = jax.nn.sigmoid(p[:, :H] + hr)
                z = jax.nn.sigmoid(p[:, H:2 * H] + hz)
                n = jnp.tanh(p[:, 2 * H:] + r * hn)
                h = (1.0 - z) * n + z * h
                return (h, h)
            h0 = jnp.zeros((B, H), x.dtype)
            _, hs = jax.lax.scan(step, h0, jnp.swapaxes(pre, 0, 1))
            return jnp.swapaxes(hs, 0, 1)

        def _bigru_layer(x, wih, whh, bih, bhh):
            fwd = _gru_dir(x, wih[0], whh[0], bih[0], bhh[0])
            bwd = _gru_dir(x[:, ::-1], wih[1], whh[1], bih[1], bhh[1])[:, ::-1]
            return jnp.concatenate([fwd, bwd], axis=-1)
        e_item = emb_item[item_id]
        pooled = jnp.max(emb_item[past_interactions], axis=1)
        e_price = emb_price[price_rank]
        e_city = emb_city[city]
        e_last = emb_item[last_item]
        e_impidx = emb_imp[impression_index]
        e_lci = emb_item[last_click_item]
        e_lcimp = emb_imp[last_click_impression]
        e_lii = emb_imp[last_interact_index]
        e_cp = emb_cp[city_platform]
        sess = jnp.concatenate([emb_item[past_interactions_sess], emb_act[past_actions_sess]], axis=2)
        sess = _bigru_layer(sess, gru_wih0, gru_whh0, gru_bih0, gru_bhh0)
        sess = _bigru_layer(sess, gru_wih1, gru_whh1, gru_bih1, gru_bhh1)
        pooled_sess = jnp.max(sess, axis=1)
        item_inter = e_item * pooled
        item_last = e_item * e_last
        item_lc = e_item * e_lci
        imp_last = e_impidx * e_lii
        emb_concat = jnp.concatenate([e_item, pooled, e_price, e_city, e_last, e_impidx], axis=1)
        s = jnp.sum(emb_concat, axis=1)
        sum_sq = (s * s)[:, None]
        sq_sum = jnp.sum(emb_concat * emb_concat, axis=1)[:, None]
        second = 0.5 * (sum_sq - sq_sum)
        sq_cont = cont_features * cont_features
        concat = jnp.concatenate([e_item, pooled, e_price, e_city, e_last, e_impidx, item_inter, item_last, pooled_sess, e_lci, e_lcimp, e_lii, item_lc, imp_last, e_cp], axis=1)
        x = _bn(concat, bn_g, bn_b)
        h = jax.nn.relu(x @ w1.T + b1)
        h = jnp.concatenate([cont_features, h, sum_sq, sq_sum, second, sq_cont, neighbor_prices], axis=1)
        h = _bn(h, bn_g, bn_b)
        h = jax.nn.relu(h @ w2.T + b2)
        return jax.nn.sigmoid(h @ wout + bout)
    y = _L0_rec_ref(r_item_id, r_past_interactions, L0_rec_mask, r_price_rank, r_city, r_last_item, r_impression_index, r_cont_features, r_past_interactions_sess, r_past_actions_sess, r_last_click_item, r_last_click_impression, r_last_interact_index, r_neighbor_prices, r_city_platform, L0_rec_emb_item, L0_rec_emb_price, L0_rec_emb_city, L0_rec_emb_imp, L0_rec_emb_act, L0_rec_emb_cp, L0_rec_gru_wih0, L0_rec_gru_whh0, L0_rec_gru_bih0, L0_rec_gru_bhh0, L0_rec_gru_wih1, L0_rec_gru_whh1, L0_rec_gru_bih1, L0_rec_gru_bhh1, L0_rec_bn_g, L0_rec_bn_b, L0_rec_w1, L0_rec_b1, L0_rec_w2, L0_rec_b2, L0_rec_wout, L0_rec_bout)
    return y

_drawn_inputs = setup_inputs


def setup_inputs(seed=0):
    import zlib

    import numpy as np

    out = dict(_drawn_inputs(seed))
    spreads = {'L0_rec_bn_g': (1.0, 0.544),
     'L0_rec_bn_b': (0.0, 0.8),
     'L0_rec_b1': (0.0, 0.8),
     'L0_rec_b2': (0.0, 0.8)}
    factors = {'r_cont_features': 3.688,
     'r_neighbor_prices': 5.371,
     'L0_rec_gru_whh0': 4.555,
     'L0_rec_gru_bih0': 8.0,
     'L0_rec_gru_bhh0': 8.0,
     'L0_rec_gru_whh1': 4.132,
     'L0_rec_gru_bih1': 8.0,
     'L0_rec_gru_bhh1': 8.0}
    for name, (base, spread) in spreads.items():
        noise = np.random.default_rng([zlib.crc32(name.encode()), seed]).standard_normal(out[name].shape)
        drawn = base * np.exp(spread * noise) if base else spread * noise
        out[name] = jnp.asarray(drawn.astype(out[name].dtype))
    for name, factor in factors.items():
        out[name] = (out[name] * factor).astype(out[name].dtype)
    return out
```

```python
from contextlib import ExitStack

import concourse.bass as bass
from concourse import mybir

ALU = mybir.AluOpType
ACT = mybir.ActivationFunctionType
F32 = mybir.dt.float32
BF16 = mybir.dt.bfloat16
I32 = mybir.dt.int32
U32 = mybir.dt.uint32

P = 128
H = 64
T = 30
B = 1024
BT = B // P
C = 2
CW = B // C
PAIRS = T // 2
PEEL = 3
NPAST = 10
FT = 15
MT = 15
H1 = 1852
N2 = 256
EPS = 1e-5
V_ITEM, V_CITY, V_CP, V_PRICE, V_IMP, V_ACT = 62500, 6250, 7500, 30, 30, 10
SMALL = T + 4
G_ITEM, G_LAST, G_LCI, G_CITY, G_CP, G_POOL = range(6)
(X_ITEM, X_POOL, X_PRICE, X_CITY, X_LAST, X_IMP, X_INTER, X_ILAST, X_SESS, X_LCI, X_LCIMP, X_LII, X_ILC,
 X_IMPL, X_CP) = range(15)
R_CONT, R_NEIGH, R_CONT2, R_SUM2, R_SQ, R_SECOND = 0, 20, 64, 96, 97, 98
N_CONT, N_NEIGH = 20, 25


def rec_kernel(nc, d, out):
    xT_dram = nc.dram_tensor("session_x_T", (T, P, B), F32, kind="Internal").ap()
    h0_dram = nc.dram_tensor("layer0_h_T", (T, P, B), F32, kind="Internal").ap()
    small_dram = nc.dram_tensor("small_ids", (SMALL, B), BF16, kind="Internal").ap()

    ctx = ExitStack()
    with ctx:
        def sb(name, shape, dt=F32):
            return ctx.enter_context(nc.sbuf_tensor(name, shape, dt))

        def sem(name):
            return ctx.enter_context(nc.semaphore(name))

        ident = sb("ident", [P, P])
        ones = sb("ones", [P, 1])
        cmp_act = sb("cmp_act", [2 * 32, 1])
        cmp_emb = sb("cmp_emb", [90, 1])
        small_lim = sb("small_lim", [SMALL, 2])
        wx = [sb(f"wx{l}", [P, 2, 3, H]) for l in range(2)]
        wa = sb("wa", [P, 2, 3, H])
        wh = [sb(f"wh{l}", [P, 3, 2 * H]) for l in range(2)]
        bih = sb("bih", [P, 2, 3])
        bhh = sb("bhh", [P, 2, 3])
        brz = sb("brz", [P, 2, 3])
        act_T = sb("act_T", [P, V_ACT])
        act_tab = sb("act_tab", [64, 3, 2 * H], BF16)
        emb_s = sb("emb_s", [30, 2, P])
        emb_tab = sb("emb_tab", [90, 2, P], BF16)
        bn1 = sb("bn1", [P, 2, FT])
        bn2 = sb("bn2", [P, 2, MT + 1])
        b1 = sb("b1", [P, MT])
        b2 = sb("b2", [P, 2])
        wout = sb("wout", [P, 2])
        bout = sb("bout", [1, 1])
        prime = sb("prime", [1, 8])
        NCOL = T + NPAST + 5
        ids = sb("ids", [P, NCOL * BT], I32)
        ids_ok = sb("ids_ok", [P, NCOL * BT], I32)
        ids_now = sb("ids_now", [P, 2, 2 * BT], I32)
        h = sb("h", [P, C, CW])
        r = sb("r", [P, C, CW])
        z = sb("z", [P, C, CW])
        n = sb("n", [P, C, CW])
        onehot = sb("onehot", [64, 2, B], BF16)
        act_rows = sb("act_rows", [64, 2, B], BF16)
        XH = sb("XH", [P, FT, B])
        E = sb("E", [P, 6, BT, P])
        work = sb("work", [P, MT * B])
        w1r = sb("w1r", [P, 2, FT, P])
        other = sb("other", [P, B])
        mv1 = sb("mv1", [P, FT, 2])
        mv2 = sb("mv2", [P, MT + 1, 2])
        st = sb("st", [P, MT + 1, 2, 6])
        std = sb("std", [P, MT + 1])
        ac = sb("ac", [P, 2, MT + 1])
        tmp = sb("tmp", [P, MT + 1])
        xs = work[:, 0:4 * B].rearrange("p (par f b) -> p par f b", par=2, f=2)
        xe = work[:, 4 * B:8 * B].rearrange("p (par f b) -> p par f b", par=2, f=2)
        ring = work[:, 8 * B:12 * B].rearrange("p (par f t e) -> p par f t e", par=2, f=2, t=BT)
        t_buf = work[:, 12 * B:13 * B].rearrange("p (c b) -> p c b", c=C)
        zh = work[:, 13 * B:14 * B].rearrange("p (c b) -> p c b", c=C)
        h1 = work[:].rearrange("p (m b) -> p m b", m=MT)
        small_i = w1r[0:SMALL, 0, 0:8, :].rearrange("p a b -> p (a b)").bitcast(I32)
        small_f = XH[0:SMALL, 0, :]
        small_g = XH[0:SMALL, 1, :]
        small_b = XH[0:SMALL, 2, 0:B // 2].bitcast(BF16)
        ids_neg = XH[:, 3, 0:NCOL * BT]
        part_rest = XH[0:V_ACT, 4, 0:2 * 6 * H].rearrange("p (k n) -> p k n", k=2)
        part = XH[0:V_ACT, 5, 0:3 * 6 * H // 2].bitcast(BF16).rearrange("p (k n) -> p k n", k=3)
        emb_rest = XH[0:30, 9, 0:2 * 2 * P].rearrange("p (k e n) -> p k e n", k=2, e=2)
        emb_part = XH[0:30, 10, 0:3 * P].bitcast(BF16).rearrange("p (k e n) -> p k e n", k=3, e=2)
        feat_rows = XH[0:90, 6:8, :].rearrange("p a b -> p (a b)").bitcast(BF16).rearrange("p (k b) -> p k b", k=4)
        feat_oh = XH[0:90, 12:14, :].rearrange("p a b -> p (a b)").bitcast(BF16).rearrange("p (k b) -> p k b", k=4)
        eflat = E[:].rearrange("p s t e -> p (s t e)")
        w2s = eflat[:, 0:16 * N2].rearrange("p (k n) -> p k n", k=16)
        h2 = eflat[:, 16 * N2:16 * N2 + 2 * B].rearrange("p (m b) -> p m b", m=2)
        sq = work[:, 0:B]
        srow = work[0:1, B:4 * B].rearrange("p (k b) -> p k b", k=3)
        s_sb = work[0:1, 4 * B:5 * B]
        y = work[0:1, 0:B]

        ps = ctx.enter_context(nc.psum_tensor("ps", [P, 8, CW], F32))
        ps_r, ps_z, ps_xn = ps[:, 0:2, :], ps[:, 2:4, :], ps[:, 4:6, :]
        ps_hn, ps_t = ps[:, 6, :], ps[:, 7, :]

        s_pre_w = sem("weights_loaded")
        s_ids = sem("ids_loaded")
        s_idok = sem("ids_clamped")
        s_small = sem("small_ids_stored")
        s_dve = sem("dve_setup")
        s_parts = sem("act_table_parts_placed")
        s_tabps = sem("act_table_product")
        s_now = sem("pair_ids_copied")
        s_gath = [sem(f"pair_gathered{i}") for i in range(2)]
        s_fgath = sem("features_gathered")
        s_fring = sem("past_column_gathered")
        s_fpool = sem("past_column_pooled")
        s_fnow = sem("past_ids_copied")
        s_t = sem("quarter_transposed")
        s_ev = sem("quarter_evacuated")
        s_xd = [sem(f"pair_x_stored{i}") for i in range(2)]
        s_xs = [sem(f"step_x_loaded{i}") for i in range(2)]
        s_ar = [sem(f"step_actions_loaded{i}") for i in range(2)]
        s_oh = sem("onehot_built")
        s_px = sem("input_products_done")
        s_pr, s_phn, s_pz = sem("r_product"), sem("hn_product"), sem("z_product")
        s_r, s_z, s_n = sem("r_gate"), sem("z_gate"), sem("n_gate")
        s_t1, s_t2, s_zh, s_zc, s_m, s_h = (sem("r_times_hn"), sem("n_argument"), sem("z_times_h"),
                                            sem("banks_free"), sem("n_part"), sem("h_new"))
        s_hs = [sem(f"h_stored{c}") for c in range(C)]
        s_max = sem("session_max")
        s_ft, s_fe = sem("feature_product"), sem("feature_evacuated")
        s_frow = sem("feature_rows_loaded")
        s_foh = sem("feature_onehots")
        s_fx = sem("feature_vector_ops")
        s_sq = sem("feature_square")
        s_sqp = sem("feature_square_summed")
        s_sum = sem("row_sums")
        s_oth = sem("other_rows")
        s_oth2 = sem("other_sums_placed")
        s_c2 = sem("cont_squared")
        s_sqrt = sem("deviation")
        s_app = sem("features_normalised")
        s_w1 = [sem(f"w1_loaded{i}") for i in range(2)]
        s_m1 = sem("dense1_product")
        s_m1e = sem("dense1_relu")
        s_st = sem("dense1_stats")
        s_w2l = sem("w2_loaded")
        s_w2 = sem("w2_scaled")
        s_m2 = sem("dense2_product")
        s_b2 = sem("dense2_bias")
        s_m2e = sem("dense2_relu")
        s_y = sem("logit")
        s_ye = sem("output_ready")
        s_out = sem("output_stored")
        s_tick_pool, s_tick_sp = sem("tick_pool"), sem("tick_sp")

        N_W = 19
        L1N = 2 * T

        def col(j):
            return ids_ok[:, j * BT:(j + 1) * BT]

        block = ctx.enter_context(nc.Block())

        @block.sync
        def _(sp):
            sp.dma_start(ids[:], d["ids"]).then_inc(s_ids, 16)
            sp.dma_start(small_i, d["small"]).then_inc(s_ids, 16)
            sp.dma_start(small_lim[:], d["small_lim"]).then_inc(s_ids, 16)
            for dst, src in ((ident[:], d["ident"]), (cmp_act[:], d["cmp_act"]), (cmp_emb[:], d["cmp_emb"]),
                             (wx[0][:], d["wih0"][0:P]), (wa[:], d["wih0"][P:2 * P]), (wx[1][:], d["wih1"]),
                             (bih[:], d["bih"]), (bhh[:], d["bhh"]), (act_T[:], d["act_T"]),
                             (emb_s[:, 0, :], d["emb_price"]), (emb_s[:, 1, :], d["emb_imp"]),
                             (bn1[:], d["bn1"]), (bn2[:], d["bn2"]), (b1[:], d["b1"]), (b2[:], d["b2"])):
                sp.dma_start(dst, src).then_inc(s_pre_w, 16)
            sp.wait_ge(s_dve, 1)
            for l in range(2):
                for f in range(2):
                    sp.dma_start(wh[l][f * H:(f + 1) * H, :, f * H:(f + 1) * H], d[f"whh{l}"][f]).then_inc(s_pre_w, 16)
            sp.wait_ge(s_idok, 4)
            sp.dma_start(small_dram, small_b).then_inc(s_small, 16)
            sp.wait_ge(s_tabps, 2)
            for k in range(3):
                for f in range(2):
                    sp.dma_start(act_tab[32 * f + 10 * k:32 * f + 10 * k + 10, :, f * H:(f + 1) * H],
                                 part[:, k, :].rearrange("p (f g n) -> p f g n", f=2, g=3)[:, f]).then_inc(s_parts, 16)
                sp.dma_start(emb_tab[30 * k:30 * k + 30, :, :], emb_part[:, k, :, :]).then_inc(s_parts, 16)

            def load0(S, par, u):
                sp.dma_start(xs[:, par, 0, :], xT_dram[S]).then_inc(s_xs[par], 16)
                sp.dma_start(xs[:, par, 1, :], xT_dram[T - 1 - S]).then_inc(s_xs[par], 16)
                sp.dma_start(act_rows[0:32, par, :], small_dram[S].partition_broadcast(32)).then_inc(s_ar[par], 16)
                sp.dma_start(act_rows[32:64, par, :], small_dram[T - 1 - S].partition_broadcast(32)).then_inc(s_ar[par], 16)

            def load1(S, par):
                sp.dma_start(xs[:, par, 0, :], h0_dram[S]).then_inc(s_xs[par], 16)
                sp.dma_start(xs[:, par, 1, :], h0_dram[T - 1 - S]).then_inc(s_xs[par], 16)

            def store_h(S):
                for c in range(C):
                    sp.wait_ge(s_h, 2 * S + c + 3)
                    sp.dma_start(h0_dram[S, 0:H, c * CW:(c + 1) * CW], h[0:H, c, :]).then_inc(s_hs[c], 16)
                    sp.dma_start(h0_dram[T - 1 - S, H:P, c * CW:(c + 1) * CW], h[H:P, c, :]).then_inc(s_hs[c], 16)

            sp.wait_ge(s_small, 16)
            sp.wait_ge(s_xd[0], 32)
            load0(0, 0, 0)
            with sp.Fori(0, (T // 2 - PEEL) // 2) as i:
                for u in range(2):
                    S = i * 2 + u
                    sp.wait_ge(s_xd[(u + 1) % 2], (i + (u + 1) // 2 + 1) * 32)
                    sp.wait_ge(s_px, S * 2 + 2)
                    sp.sem_inc(s_tick_sp, 1)
                    sp.wait_ge(s_oh, S + 1)
                    load0(S + 1, (u + 1) % 2, 0)
                    store_h(S)
            sp.wait_ge(s_xd[0], 32 * 8)
            sp.wait_ge(s_xd[1], 32 * 7)
            with sp.Fori((T // 2 - PEEL) // 2, T // 2 - 1) as i:
                for u in range(2):
                    S = i * 2 + u
                    sp.wait_ge(s_px, S * 2 + 2)
                    sp.sem_inc(s_tick_sp, 1)
                    sp.wait_ge(s_oh, S + 1)
                    load0(S + 1, (u + 1) % 2, 0)
                    store_h(S)
            sp.wait_ge(s_px, 2 * (T - 2) + 2)
            sp.wait_ge(s_oh, T - 1)
            load0(T - 1, 1, 0)
            store_h(T - 2)
            sp.wait_ge(s_px, 2 * (T - 1) + 2)
            store_h(T - 1)
            for c in range(C):
                sp.wait_ge(s_hs[c], 32 * T + 1)
            load1(0, 0)
            with sp.Fori(0, T // 2 - 1) as i:
                for u in range(2):
                    S = i * 2 + u
                    sp.wait_ge(s_px, S * 2 + 2 + L1N)
                    load1(S + 1, (u + 1) % 2)
            sp.wait_ge(s_px, 2 * (T - 2) + 2 + L1N)
            load1(T - 1, 1)
            for k in range(4):
                sp.dma_start(feat_rows[:, k, :], small_dram[T + k].partition_broadcast(90)).then_inc(s_frow, 16)
            sp.wait_ge(s_c2, 1)
            sp.dma_start(other[R_CONT:R_CONT + N_CONT, :], d["cont_T"]).then_inc(s_oth, 16)
            sp.dma_start(other[R_NEIGH:R_NEIGH + N_NEIGH, :], d["neigh_T"]).then_inc(s_oth, 16)
            sp.dma_start(wout[:], d["wout"]).then_inc(s_oth, 16)
            sp.dma_start(bout[:], d["bout"]).then_inc(s_oth, 16)
            for m in range(2):
                sp.dma_start(w1r[:, m], d["w1"][m]).then_inc(s_w1[m], 16)
            sp.wait_ge(s_sum, 2)
            for k, row in enumerate((R_SUM2, R_SQ, R_SECOND)):
                sp.dma_start(other[row:row + 1, :], srow[:, k, :]).then_inc(s_oth2, 16)
            sp.wait_ge(s_ft, 6)
            sp.dma_start(w2s, d["w2"]).then_inc(s_w2l, 16)
            with sp.Fori(1, MT // 2) as i:
                for u in range(2):
                    m = i * 2 + u
                    sp.wait_ge(s_m1, m * 2 - 2)
                    sp.dma_start(w1r[:, u], d["w1"][m]).then_inc(s_w1[u], 16)
            sp.wait_ge(s_m1, 2 * (MT - 1) - 2)
            sp.dma_start(w1r[:, 0], d["w1"][MT - 1]).then_inc(s_w1[0], 16)
            sp.wait_ge(s_ye, 1)
            sp.dma_start(out, y).then_inc(s_out, 16)
            sp.wait_ge(s_out, 16)

        @block.gpsimd
        def _(pool):
            pool.wait_ge(s_idok, 3)

            def gather(dst, idx, table, done):
                pool.indirect_dma_start(dst, None, table,
                                        bass.IndirectOffsetOnAxis(ap=idx.bitcast(U32), axis=0)).then_inc(done, 16)

            def gather_pair(j, par, first=False):
                nc.gpsimd.tensor_copy(ids_now[:, par, :], ids_ok[:, bass.ds(j * (2 * BT), 2 * BT)]).then_inc(s_now, 1)
                pool.wait_ge(s_now, j + 1)
                pool.sem_inc(s_tick_pool, 1)
                for f in range(2):
                    for b in range(BT):
                        gather(ring[:, par, f, b, :], ids_now[:, par, f * BT + b:f * BT + b + 1], d["emb_item"],
                               s_gath[par])

            gather_pair(0, 0)
            gather_pair(1, 1)
            with pool.Fori(1, PAIRS // 2) as i:
                for u in range(2):
                    j = i * 2 + u
                    pool.wait_ge(s_t, (j - 1) * 4)
                    gather_pair(j, u)
            pool.wait_ge(s_t, (PAIRS - 2) * 4)
            gather_pair(PAIRS - 1, 0)
            at = T + NPAST
            for slot, table in ((G_ITEM, "emb_item"), (G_LAST, "emb_item"), (G_LCI, "emb_item"),
                                (G_CITY, "emb_city"), (G_CP, "emb_cp")):
                for b in range(BT):
                    gather(E[:, slot, b, :], col(at + slot)[:, b:b + 1], d[table], s_fgath)
            for b in range(BT):
                gather(E[:, G_POOL, b, :], col(T)[:, b:b + 1], d["emb_item"], s_fring)
            pool.wait_ge(s_t, PAIRS * 4)
            with pool.Fori(1, NPAST) as k:
                pool.wait_ge(s_fpool, k)
                nc.gpsimd.tensor_copy(ids_now[:, 1, 0:BT], ids_ok[:, bass.ds((k + T) * BT, BT)]).then_inc(s_fnow, 1)
                pool.wait_ge(s_fnow, k)
                pool.sem_inc(s_tick_pool, 1)
                for b in range(BT):
                    gather(ring[:, 1, 0, b, :], ids_now[:, 1, b:b + 1], d["emb_item"], s_fring)

        @block.tensor
        def _(pe):
            pe.wait_ge(s_pre_w, 16 * N_W)
            pe.wait_ge(s_dve, 5)
            nc.tensor.matmul(ps_hn[0:V_ACT, 0:384], act_T[:], wa[:].rearrange("p f g n -> p (f g n)"),
                             start=True, stop=True).then_inc(s_tabps, 1)

            def transpose_quarter(q, par, w_gath, w_ev):
                if q == 0:
                    pe.wait_ge(s_gath[par], w_gath)
                pe.wait_ge(s_ev, w_ev)
                f, half = q // 2, q % 2
                for k in range(4):
                    last = nc.tensor.transpose(ps_t[:, k * P:(k + 1) * P], ring[:, par, f, 4 * half + k, :], ident[:])
                last.then_inc(s_t, 1)

            def x_product(l, c, par, N):
                pe.wait_ge(s_zc, N + 1)
                for g, bank in enumerate((ps_r, ps_z, ps_xn)):
                    for f in range(2):
                        last = nc.tensor.matmul(bank[f * H:(f + 1) * H, c, :], wx[l][:, f, g, :],
                                                xs[:, par, f, c * CW:(c + 1) * CW], start=True,
                                                stop=(l == 1 and g == 2), skip_group_check=True)
                if l == 0:
                    for g, bank in enumerate((ps_r, ps_z, ps_xn)):
                        last = nc.tensor.matmul(bank[:, c, :], act_tab[:, g, :],
                                                onehot[:, par, c * CW:(c + 1) * CW], start=False, stop=(g == 2),
                                                skip_group_check=True)
                last.then_inc(s_px, 1)

            def h_product(l, c, N):
                pe.wait_ge(s_h, N + 1 + 2 * l)
                nc.tensor.matmul(ps_r[:, c, :], wh[l][:, 0, :], h[:, c, :], start=False, stop=True,
                                 skip_group_check=True).then_inc(s_pr, 1)
                pe.wait_ge(s_t1, N + 1)
                nc.tensor.matmul(ps_hn, wh[l][:, 2, :], h[:, c, :], start=True, stop=True).then_inc(s_phn, 1)
                nc.tensor.matmul(ps_z[:, c, :], wh[l][:, 1, :], h[:, c, :], start=False, stop=True,
                                 skip_group_check=True).then_inc(s_pz, 1)

            for j in range(PEEL):
                for q in range(4):
                    transpose_quarter(q, j % 2, 256 * (j // 2 + 1), 4 * j + q + 1)
            pe.wait_ge(s_parts, 16 * 9)
            with pe.Fori(0, (T // 2 - PEEL) // 2) as i:
                for u in range(2):
                    S = i * 2 + u
                    j, jp = S + PEEL, (u + PEEL) % 2
                    wg = (i + (u + PEEL) // 2 + 1) * 256
                    pe.wait_ge(s_xs[u], (i + 1) * 32)
                    pe.wait_ge(s_oh, S + 1)
                    x_product(0, 0, u, S * 2)
                    transpose_quarter(0, jp, wg, j * 4 + 1)
                    h_product(0, 0, S * 2)
                    transpose_quarter(1, jp, wg, j * 4 + 2)
                    x_product(0, 1, u, S * 2 + 1)
                    transpose_quarter(2, jp, wg, j * 4 + 3)
                    h_product(0, 1, S * 2 + 1)
                    transpose_quarter(3, jp, wg, j * 4 + 4)
            with pe.Fori((T // 2 - PEEL) // 2, T // 2) as i:
                for u in range(2):
                    S = i * 2 + u
                    pe.wait_ge(s_xs[u], (i + 1) * 32)
                    pe.wait_ge(s_oh, S + 1)
                    for c in range(C):
                        x_product(0, c, u, S * 2 + c)
                        h_product(0, c, S * 2 + c)
            with pe.Fori(T // 2, T) as i:
                for u in range(2):
                    S = i * 2 + u
                    pe.wait_ge(s_xs[u], (i + 1) * 32)
                    for c in range(C):
                        x_product(1, c, u, S * 2 + c)
                        h_product(1, c, S * 2 + c)

            pe.wait_ge(s_fgath, 16 * BT * 5)
            pe.wait_ge(s_fpool, NPAST)
            pe.wait_ge(s_max, 2 * T + 2)
            for k, (slot, x) in enumerate(FEATURES):
                if k >= 4:
                    pe.wait_ge(s_fe, k - 3)
                bk = 2 * (k % 4)
                for half in range(2):
                    bank = ps[:, bk + half, :]
                    if k < 6:
                        for q in range(4):
                            last = nc.tensor.transpose(bank[:, q * P:(q + 1) * P], E[:, slot, 4 * half + q, :], ident[:])
                    else:
                        if k == 6:
                            pe.wait_ge(s_foh, 1)
                        last = nc.tensor.matmul(bank, emb_tab[:, slot, :], feat_oh[:, k - 6, half * CW:(half + 1) * CW],
                                                start=True, stop=True)
                last.then_inc(s_ft, 1)
            pe.wait_ge(s_fe, 10)
            for k in range(6):
                for half in range(2):
                    last = nc.tensor.matmul(ps[0:1, half, :], ones[:], XH[:, k, half * CW:(half + 1) * CW],
                                            start=(k == 0), stop=(k == 5))
            for k in range(6):
                pe.wait_ge(s_sq, k + 1)
                for half in range(2):
                    last = nc.tensor.matmul(ps[0:1, 2 + half, :], ones[:], sq[:, half * CW:(half + 1) * CW],
                                            start=(k == 0), stop=(k == 5))
                last.then_inc(s_sqp, 1)
            pe.wait_ge(s_app, 2)

            def dense1(m, par, w_w1):
                pe.wait_ge(s_w1[par], w_w1)
                for half in range(2):
                    bank = ps[:, 4 + 2 * par + half, :]
                    for k in range(FT):
                        last = nc.tensor.matmul(bank, w1r[:, par, k, :], XH[:, k, half * CW:(half + 1) * CW],
                                                start=(k == 0), stop=(k == FT - 1))
                    last.then_inc(s_m1, 1)

            dense1(0, 0, 16)
            dense1(1, 1, 16)
            with pe.Fori(1, MT // 2) as i:
                for u in range(2):
                    pe.wait_ge(s_m1e, (i * 2 + u - 1) * 2)
                    dense1(i * 2 + u, u, (i + 1) * 16)
            pe.wait_ge(s_m1e, (MT - 2) * 2)
            dense1(MT - 1, 0, 16 * (MT // 2 + 1))
            pe.wait_ge(s_w2, 1)
            for m in range(2):
                for k in range(MT + 1):
                    last = nc.tensor.matmul(ps[:, m, 0:1], w2s[:, k, m * P:(m + 1) * P], std[:, k:k + 1],
                                            start=(k == 0), stop=(k == MT))
            last.then_inc(s_b2, 1)
            pe.wait_ge(s_w2, 2)
            for m in range(2):
                for half in range(2):
                    for k in range(MT + 1):
                        rhs = h1[:, k, half * CW:(half + 1) * CW] if k < MT else other[:, half * CW:(half + 1) * CW]
                        last = nc.tensor.matmul(ps[:, 4 + 2 * m + half, :], w2s[:, k, m * P:(m + 1) * P], rhs,
                                                start=(k == 0), stop=(k == MT))
                    last.then_inc(s_m2, 1)
            pe.wait_ge(s_m2e, 4)
            for half in range(2):
                for m in range(2):
                    last = nc.tensor.matmul(ps[0:1, 2 + half, :], wout[:, m:m + 1], h2[:, m, half * CW:(half + 1) * CW],
                                            start=(m == 0), stop=(m == 1))
            last.then_inc(s_y, 1)

        @block.scalar
        def _(act):
            act.wait_ge(s_pre_w, 16 * N_W)
            act.wait_ge(s_dve, 5)

            def evacuate(j, q, par):
                act.wait_ge(s_t, j * 4 + q + 1)
                nc.scalar.activation(xe[:, par, q // 2, (q % 2) * CW:(q % 2 + 1) * CW], ps_t, ACT.Copy).then_inc(s_ev, 1)

            def store_pair(j, par):
                act.wait_ge(s_ev, j * 4 + 5)
                act.dma_start(xT_dram[j], xe[:, par, 0, :]).then_inc(s_xd[par], 16)
                act.dma_start(xT_dram[T - 1 - j], xe[:, par, 1, :]).then_inc(s_xd[par], 16)

            def gates(l, c, N):
                act.wait_ge(s_pr, N + 1)
                nc.scalar.activation(r[:, c, :], ps_r[:, c, :], ACT.Sigmoid, bias=brz[:, l, 0:1]).then_inc(s_r, 1)
                act.wait_ge(s_pz, N + 1)
                nc.scalar.activation(z[:, c, :], ps_z[:, c, :], ACT.Sigmoid, bias=brz[:, l, 1:2]).then_inc(s_z, 1)

            def new(l, c, N):
                act.wait_ge(s_t2, N + 1)
                nc.scalar.activation(n[:, c, :], t_buf[:, c, :], ACT.Tanh, bias=bih[:, l, 2:3]).then_inc(s_n, 1)

            for j in range(PEEL):
                if j >= 2:
                    act.wait_ge(s_xd[j % 2], 32 * (j // 2))
                for q in range(4):
                    evacuate(j, q, j % 2)
                store_pair(j, j % 2)
            with act.Fori(0, (T // 2 - PEEL) // 2) as i:
                for u in range(2):
                    S = i * 2 + u
                    j, jp = S + PEEL, (u + PEEL) % 2
                    act.wait_ge(s_xd[jp], (i + (u + PEEL) // 2) * 32)
                    evacuate(j, 0, jp)
                    gates(0, 0, S * 2)
                    evacuate(j, 1, jp)
                    new(0, 0, S * 2)
                    evacuate(j, 2, jp)
                    gates(0, 1, S * 2 + 1)
                    evacuate(j, 3, jp)
                    new(0, 1, S * 2 + 1)
                    store_pair(j, jp)
            for l, first, end in ((0, (T // 2 - PEEL) // 2, T // 2), (1, T // 2, T)):
                with act.Fori(first, end) as i:
                    for u in range(2):
                        for c in range(C):
                            gates(l, c, i * 4 + 2 * u + c)
                            new(l, c, i * 4 + 2 * u + c)

            for k, (slot, x) in enumerate(FEATURES):
                act.wait_ge(s_ft, k + 1)
                bk = 2 * (k % 4)
                nc.scalar.activation(XH[:, x, :], ps[:, bk:bk + 2, :].rearrange("p a b -> p (a b)"), ACT.Copy)\
                    .then_inc(s_fe, 1)
            act.wait_ge(s_fe, 10)
            for k in range(6):
                if k:
                    act.wait_ge(s_sqp, k)
                nc.scalar.activation(sq, XH[:, k, :], ACT.Square).then_inc(s_sq, 1)
            act.wait_ge(s_oth, 64)
            nc.scalar.activation(other[R_CONT2:R_CONT2 + N_CONT, :], other[R_CONT:R_CONT + N_CONT, :], ACT.Square)\
                .then_inc(s_c2, 1)
            act.wait_ge(s_fx, 6)
            nc.scalar.activation(tmp[:, 0:FT], tmp[:, 0:FT], ACT.Sqrt).then_inc(s_sqrt, 1)
            act.wait_ge(s_fx, 10)
            for k in range(1, FT, 2):
                last = nc.scalar.activation(XH[:, k, :], XH[:, k, :], ACT.Identity, bias=std[:, k:k + 1],
                                            scale=ac[:, 0, k:k + 1])
            last.then_inc(s_app, 1)

            def relu1(m, par):
                for half in range(2):
                    act.wait_ge(s_m1, m * 2 + half + 1)
                    nc.scalar.activation(h1[:, m, half * CW:(half + 1) * CW], ps[:, 4 + 2 * par + half, :], ACT.Relu,
                                         bias=b1[:, bass.ds(m, 1)]).then_inc(s_m1e, 1)

            act.wait_ge(s_oth2, 48)
            with act.Fori(0, MT // 2) as i:
                for u in range(2):
                    relu1(i * 2 + u, u)
            relu1(MT - 1, 0)
            act.wait_ge(s_fx, 13)
            nc.scalar.activation(tmp[:], tmp[:], ACT.Sqrt).then_inc(s_sqrt, 1)
            act.wait_ge(s_fx, 18)
            for m in range(2):
                for half in range(2):
                    act.wait_ge(s_m2, 2 * m + half + 1)
                    nc.scalar.activation(h2[:, m, half * CW:(half + 1) * CW], ps[:, 4 + 2 * m + half, :], ACT.Relu,
                                         bias=tmp[:, m:m + 1]).then_inc(s_m2e, 1)
            act.wait_ge(s_y, 1)
            nc.scalar.activation(y, ps[0:1, 2:4, :].rearrange("p a b -> p (a b)"), ACT.Sigmoid, bias=bout[:])\
                .then_inc(s_ye, 1)

        @block.vector
        def _(dve):
            V = nc.vector
            for l in range(2):
                last = V.memset(wh[l][:], 0.0)
            last.then_inc(s_dve, 1)
            V.memset(act_tab[:], 0.0)
            V.memset(ones[:], 1.0)
            V.memset(h[:], 0.0).then_inc(s_h, 2)
            V.memset(prime[:, 0:1], 0.0).then_inc(s_zc, 2)
            V.memset(prime[:, 1:2], 0.0).then_inc(s_t1, 1)
            V.memset(prime[:, 2:3], 0.0).then_inc(s_ev, 1)
            for c in range(C):
                V.memset(prime[:, 6 + c:7 + c], 0.0).then_inc(s_hs[c], 1)
            V.memset(prime[:, 5:6], 0.0).then_inc(s_fpool, 1)
            V.memset(prime[:, 3:4], 0.0).then_inc(s_px, 2)
            V.memset(XH[:, X_SESS, :], -3.0e38).then_inc(s_max, 2)
            dve.wait_ge(s_ids, 48)
            n_item = (T + NPAST + 3) * BT
            ranges = ((0, n_item, V_ITEM), (n_item, n_item + BT, V_CITY), (n_item + BT, n_item + 2 * BT, V_CP))
            for a, b, v in ranges:
                last = V.tensor_scalar(ids_neg[:, a:b], ids[:, a:b], 0.0, float(v), ALU.is_lt, ALU.mult)
            V.tensor_scalar(small_f, small_i, 0.0, small_lim[:, 0:1], ALU.is_lt, ALU.mult).then_inc(s_idok, 1)
            dve.wait_ge(s_idok, 1)
            V.tensor_tensor(ids_neg, ids[:], ids_neg, ALU.add)
            V.tensor_tensor(small_g, small_i, small_f, ALU.add).then_inc(s_idok, 1)
            dve.wait_ge(s_idok, 2)
            for a, b, v in ranges:
                last = V.tensor_scalar(ids_ok[:, a:b], ids_neg[:, a:b], 0.0, float(v - 1), ALU.max, ALU.min)
            last.then_inc(s_idok, 1)
            V.tensor_scalar(small_b, small_g, 0.0, small_lim[:, 1:2], ALU.max, ALU.min).then_inc(s_idok, 1)
            dve.wait_ge(s_pre_w, 16 * N_W)
            V.tensor_tensor(brz[:], bih[:], bhh[:], ALU.add).then_inc(s_dve, 4)
            dve.wait_ge(s_tabps, 1)
            count = [5]

            def link(ins):
                ins.then_inc(s_dve, 1)
                count[0] += 1
                dve.wait_ge(s_dve, count[0])

            for parts, rest, src in ((part, part_rest, ps_hn[0:V_ACT, 0:384]), (emb_part, emb_rest, emb_s[:])):
                link(V.tensor_copy(parts[:, 0], src))
                link(V.tensor_tensor(rest[:, 0], src, parts[:, 0], ALU.subtract))
                link(V.tensor_copy(parts[:, 1], rest[:, 0]))
                link(V.tensor_tensor(rest[:, 1], rest[:, 0], parts[:, 1], ALU.subtract))
                link(V.tensor_copy(parts[:, 2], rest[:, 1]))
            V.memset(prime[:, 4:5], 0.0).then_inc(s_tabps, 1)

            def build_onehot(S, par, w_rows):
                dve.wait_ge(s_ar[par], w_rows)
                dve.wait_ge(s_px, S * 2)
                V.tensor_scalar(onehot[:, par, :], act_rows[:, par, :], cmp_act[:], None, ALU.is_equal).then_inc(s_oh, 1)

            def cell(l, c, N, w_store):
                dve.wait_ge(s_r, N + 1)
                dve.wait_ge(s_phn, N + 1)
                V.scalar_tensor_tensor(t_buf[:, c, :], ps_hn, bhh[:, l, 2:3], r[:, c, :], ALU.add, ALU.mult)\
                    .then_inc(s_t1, 1)
                dve.wait_ge(s_t1, N + 2)
                V.tensor_tensor(t_buf[:, c, :], t_buf[:, c, :], ps_xn[:, c, :], ALU.add).then_inc(s_t2, 1)
                dve.wait_ge(s_z, N + 1)
                V.tensor_tensor(zh[:, c, :], z[:, c, :], h[:, c, :], ALU.mult).then_inc(s_zh, 1)
                dve.wait_ge(s_zh, N + 1)
                V.tensor_scalar(z[:, c, :], z[:, c, :], -1.0, 1.0, ALU.mult, ALU.add).then_inc(s_zc, 1)
                dve.wait_ge(s_zc, N + 3)
                dve.wait_ge(s_n, N + 1)
                V.tensor_tensor(n[:, c, :], n[:, c, :], z[:, c, :], ALU.mult).then_inc(s_m, 1)
                dve.wait_ge(s_m, N + 1)
                if w_store is not None:
                    dve.wait_ge(s_hs[c], w_store)
                V.tensor_tensor(h[:, c, :], n[:, c, :], zh[:, c, :], ALU.add).then_inc(s_h, 1)

            build_onehot(0, 0, 32)
            with dve.Fori(0, T // 2 - 1) as i:
                for u in range(2):
                    S = i * 2 + u
                    cell(0, 0, S * 2, S * 32 + 1)
                    build_onehot(S + 1, (u + 1) % 2, (i + (u + 1) // 2 + 1) * 32)
                    cell(0, 1, S * 2 + 1, S * 32 + 1)
            cell(0, 0, 2 * (T - 2), 32 * (T - 2) + 1)
            build_onehot(T - 1, 1, 32 * (T // 2))
            cell(0, 1, 2 * (T - 2) + 1, 32 * (T - 2) + 1)
            for c in range(C):
                cell(0, c, 2 * (T - 1) + c, 32 * (T - 1) + 1)
            for c in range(C):
                dve.wait_ge(s_hs[c], 32 * T + 1)
            V.memset(h[:], 0.0).then_inc(s_h, 2)

            def cell_max(c, N):
                cell(1, c, N, None)
                dve.wait_ge(s_h, N + 5)
                dve.wait_ge(s_max, N - (2 * T - 2))
                V.tensor_tensor(XH[:, X_SESS, c * CW:(c + 1) * CW], XH[:, X_SESS, c * CW:(c + 1) * CW],
                                h[:, c, :], ALU.max).then_inc(s_max, 1)

            with dve.Fori(T // 2, T // 2 + NPAST - 1) as i:
                for u in range(2):
                    for c in range(C):
                        cell_max(c, i * 4 + 2 * u + c)
                dve.wait_ge(s_fring, (i - (T // 2 - 2)) * (16 * BT))
                dve.wait_ge(s_fpool, i - (T // 2 - 1))
                V.tensor_tensor(E[:, G_POOL], E[:, G_POOL], ring[:, 1, 0], ALU.max).then_inc(s_fpool, 1)
            with dve.Fori(T // 2 + NPAST - 1, T) as i:
                for u in range(2):
                    for c in range(C):
                        cell_max(c, i * 4 + 2 * u + c)

            V.memset(other[:], 0.0).then_inc(s_c2, 1)
            dve.wait_ge(s_frow, 64)
            V.tensor_scalar(feat_oh[:, :, :], feat_rows[:, :, :], cmp_emb[:], None, ALU.is_equal).then_inc(s_foh, 1)
            dve.wait_ge(s_fe, 10)
            dve.wait_ge(s_foh, 1)
            for o, a, b in ((X_INTER, X_ITEM, X_POOL), (X_ILAST, X_ITEM, X_LAST), (X_ILC, X_ITEM, X_LCI),
                            (X_IMPL, X_IMP, X_LII)):
                last = V.tensor_tensor(XH[:, o, :], XH[:, a, :], XH[:, b, :], ALU.mult)
            last.then_inc(s_fx, 1)
            dve.wait_ge(s_sqp, 6)
            V.tensor_copy(s_sb, ps[0:1, 0:2, :].rearrange("p a b -> p (a b)"))
            V.tensor_copy(srow[:, 1, :], ps[0:1, 2:4, :].rearrange("p a b -> p (a b)")).then_inc(s_sum, 1)
            dve.wait_ge(s_sum, 1)
            V.tensor_tensor(srow[:, 0, :], s_sb, s_sb, ALU.mult).then_inc(s_fx, 1)
            dve.wait_ge(s_fx, 2)
            V.tensor_tensor(srow[:, 2, :], srow[:, 0, :], srow[:, 1, :], ALU.subtract).then_inc(s_fx, 1)
            dve.wait_ge(s_fx, 3)
            V.tensor_scalar(srow[:, 2, :], srow[:, 2, :], 0.5, None, ALU.mult).then_inc(s_sum, 1)

            def stats(src, k):
                for half in range(2):
                    last = V.bn_stats(st[:, k, half, :], src[:, half * CW:(half + 1) * CW])
                return last

            def fold(mv, bn, count, w):
                V.tensor_scalar(tmp[:, 0:count], mv[:, 0:count, 1], EPS, None, ALU.add).then_inc(s_fx, 1)
                dve.wait_ge(s_sqrt, 1 if w == 6 else 2)
                V.reciprocal(std[:, 0:count], tmp[:, 0:count]).then_inc(s_fx, 1)
                dve.wait_ge(s_fx, w + 1)
                V.tensor_tensor(ac[:, 0, 0:count], std[:, 0:count], bn[:, 0, 0:count], ALU.mult).then_inc(s_fx, 1)
                dve.wait_ge(s_fx, w + 2)
                V.tensor_tensor(ac[:, 1, 0:count], ac[:, 0, 0:count], mv[:, 0:count, 0], ALU.mult).then_inc(s_fx, 1)
                dve.wait_ge(s_fx, w + 3)
                V.tensor_tensor(std[:, 0:count], bn[:, 1, 0:count], ac[:, 1, 0:count], ALU.subtract).then_inc(s_fx, 1)

            for k in range(FT):
                last = stats(XH[:, k, :], k)
            last.then_inc(s_fx, 1)
            dve.wait_ge(s_fx, 4)
            for k in range(FT):
                last = V.bn_aggr(mv1[:, k, :], st[:, k, :, :].rearrange("p a b -> p (a b)"))
            last.then_inc(s_fx, 1)
            dve.wait_ge(s_fx, 5)
            fold(mv1, bn1, FT, 6)
            dve.wait_ge(s_fx, 10)
            for k in range(0, FT, 2):
                last = V.tensor_scalar(XH[:, k, :], XH[:, k, :], ac[:, 0, k:k + 1], std[:, k:k + 1], ALU.mult, ALU.add)
            last.then_inc(s_app, 1)
            dve.wait_ge(s_oth2, 48)
            dve.wait_ge(s_c2, 2)
            stats(other, MT)
            with dve.Fori(0, MT) as m:
                for half in range(2):
                    dve.wait_ge(s_m1e, m * 2 + half + 1)
                    V.bn_stats(st[:, m, half, :], h1[:, m, half * CW:(half + 1) * CW]).then_inc(s_st, 1)
            dve.wait_ge(s_st, 2 * MT)
            dve.wait_ge(s_app, 2)
            V.memset(prime[:, 6:7], 0.0).then_inc(s_fx, 1)
            dve.wait_ge(s_fx, 11)
            for k in range(MT + 1):
                last = V.bn_aggr(mv2[:, k, :], st[:, k, :, :].rearrange("p a b -> p (a b)"))
            last.then_inc(s_fx, 1)
            dve.wait_ge(s_fx, 12)
            fold(mv2, bn2, MT + 1, 13)
            dve.wait_ge(s_fx, 17)
            V.memset(prime[:, 7:8], 0.0).then_inc(s_w2, 1)
            dve.wait_ge(s_b2, 1)
            V.tensor_tensor(tmp[:, 0:2], ps[:, 0:2, 0], b2[:], ALU.add).then_inc(s_fx, 1)
            for k in range(MT + 1):
                last = V.tensor_scalar(w2s[:, k, :], w2s[:, k, :], ac[:, 0, k:k + 1], None, ALU.mult)
            last.then_inc(s_w2, 1)


FEATURES = ((G_ITEM, X_ITEM), (G_POOL, X_POOL), (G_LAST, X_LAST), (G_LCI, X_LCI), (G_CITY, X_CITY), (G_CP, X_CP),
            (0, X_PRICE), (1, X_IMP), (1, X_LCIMP), (1, X_LII))


def kernel(**a):
    import numpy as np
    import concourse.bacc as bacc
    from concourse import mybir
    from concourse.bass_utils import run_bass_kernel_spmd

    v = {k: np.asarray(x) for k, x in a.items()}

    def w(name):
        return v["L0_rec_" + name]

    def tiles(x):
        x = x.reshape(B, -1)
        return x.reshape(BT, P, -1).transpose(1, 2, 0)

    sess = v["r_past_interactions_sess"]
    order = [t for j in range(PAIRS) for t in (j, T - 1 - j)]
    cols = [tiles(sess[:, order]), tiles(v["r_past_interactions"])]
    cols += [tiles(v[k]) for k in ("r_item_id", "r_last_item", "r_last_click_item", "r_city", "r_city_platform")]
    ids = np.concatenate(cols, axis=1).reshape(P, -1)
    small = np.concatenate([v["r_past_actions_sess"].T] + [v[k][None, :] for k in (
        "r_price_rank", "r_impression_index", "r_last_click_impression", "r_last_interact_index")], axis=0)
    vocab = np.array([V_ACT] * T + [V_PRICE, V_IMP, V_IMP, V_IMP], np.float32)
    row = np.arange(64)

    def wih(x):
        return x.transpose(2, 0, 1).reshape(x.shape[2], 2, 3, H)

    def gates(x0, x1):
        return np.stack([x.reshape(2, 3, H).transpose(0, 2, 1).reshape(P, 3) for x in (x0, x1)], axis=1)

    def other(x, axis):
        x = np.moveaxis(x, axis, 0)
        res = np.zeros((MT * P + P,) + x.shape[1:], x.dtype)
        res[0:H1] = x[N_CONT:N_CONT + H1]
        o = MT * P
        e = N_CONT + H1
        res[o + R_CONT:o + R_CONT + N_CONT] = x[0:N_CONT]
        for k, dst in enumerate((R_SUM2, R_SQ, R_SECOND)):
            res[o + dst] = x[e + k]
        res[o + R_CONT2:o + R_CONT2 + N_CONT] = x[e + 3:e + 3 + N_CONT]
        res[o + R_NEIGH:o + R_NEIGH + N_NEIGH] = x[e + 3 + N_CONT:]
        return res

    w1 = np.zeros((MT * P, FT * P), np.float32)
    w1[0:H1] = w("w1")
    b1 = np.zeros((MT * P,), np.float32)
    b1[0:H1] = w("b1")
    arrays = {
        "ids": ids,
        "small": small,
        "small_lim": np.stack([vocab, vocab - 1], axis=1),
        "ident": np.eye(P, dtype=np.float32),
        "cmp_act": np.where(row % 32 < 30, row % 32 % 10, -1).astype(np.float32)[:, None],
        "cmp_emb": (np.arange(90) % 30).astype(np.float32)[:, None],
        "wih0": wih(w("gru_wih0")),
        "wih1": wih(w("gru_wih1")),
        "whh0": wih(w("gru_whh0")).transpose(1, 0, 2, 3),
        "whh1": wih(w("gru_whh1")).transpose(1, 0, 2, 3),
        "bih": gates(w("gru_bih0"), w("gru_bih1")),
        "bhh": gates(w("gru_bhh0"), w("gru_bhh1")),
        "act_T": w("emb_act").T,
        "emb_price": w("emb_price"),
        "emb_imp": w("emb_imp"),
        "emb_item": w("emb_item"),
        "emb_city": w("emb_city"),
        "emb_cp": w("emb_cp"),
        "bn1": np.stack([w("bn_g"), w("bn_b")]).reshape(2, FT, P).transpose(2, 0, 1),
        "bn2": np.stack([other(w("bn_g"), 0), other(w("bn_b"), 0)]).reshape(2, MT + 1, P).transpose(2, 0, 1),
        "w1": w1.reshape(MT, P, FT, P).transpose(0, 3, 2, 1),
        "b1": b1.reshape(MT, P).T,
        "w2": other(w("w2"), 1).reshape(MT + 1, P, N2).transpose(1, 0, 2),
        "b2": w("b2").reshape(2, P).T,
        "wout": w("wout").reshape(2, P).T,
        "bout": w("bout").reshape(1, 1),
        "cont_T": v["r_cont_features"].T,
        "neigh_T": v["r_neighbor_prices"].T,
    }
    arrays = {k: np.ascontiguousarray(x) for k, x in arrays.items()}
    nc = bacc.Bacc("TRN2", target_bir_lowering=False, num_devices=1)
    aps = {k: nc.dram_tensor("in_" + k, x.shape, mybir.dt.from_np(x.dtype), kind="ExternalInput").ap()
           for k, x in arrays.items()}
    out = nc.dram_tensor("out", (1, B), F32, kind="ExternalOutput").ap()
    rec_kernel(nc, aps, out)
    res = run_bass_kernel_spmd(nc, [{"in_" + k: x for k, x in arrays.items()}], core_ids=[0])
    return res.results[0]["out"].reshape(B)
```

```python
from contextlib import ExitStack

import concourse.bass as bass
from concourse import mybir

ALU = mybir.AluOpType
ACT = mybir.ActivationFunctionType
F32 = mybir.dt.float32
F32R = mybir.dt.float32r
BF16 = mybir.dt.bfloat16
I32 = mybir.dt.int32
U32 = mybir.dt.uint32

P = 128
H = 64
T = 30
B = 1024
BT = B // P
C = 2
CW = B // C
PAIRS = T // 2
PEEL = 3
NPAST = 10
FT = 15
MT = 15
H1 = 1852
N2 = 256
EPS = 1e-5
V_ITEM, V_CITY, V_CP, V_PRICE, V_IMP, V_ACT = 62500, 6250, 7500, 30, 30, 10
SMALL = T + 4
G_ITEM, G_LAST, G_LCI, G_CITY, G_CP, G_POOL = range(6)
(X_ITEM, X_POOL, X_PRICE, X_CITY, X_LAST, X_IMP, X_INTER, X_ILAST, X_SESS, X_LCI, X_LCIMP, X_LII, X_ILC,
 X_IMPL, X_CP) = range(15)
R_CONT, R_NEIGH, R_CONT2, R_SUM2, R_SQ, R_SECOND = 0, 20, 64, 96, 97, 98
N_CONT, N_NEIGH = 20, 25


def rec_kernel(nc, d, out):
    xT_dram = nc.dram_tensor("session_x_T", (T, P, B), F32, kind="Internal").ap()
    h0_dram = nc.dram_tensor("layer0_h_T", (T, P, B), F32, kind="Internal").ap()
    small_dram = nc.dram_tensor("small_ids", (SMALL, B), BF16, kind="Internal").ap()

    ctx = ExitStack()
    with ctx:
        def sb(name, shape, dt=F32):
            return ctx.enter_context(nc.sbuf_tensor(name, shape, dt))

        def sem(name):
            return ctx.enter_context(nc.semaphore(name))

        ident = sb("ident", [P, P])
        ones = sb("ones", [P, 1])
        cmp_act = sb("cmp_act", [2 * 32, 1])
        cmp_emb = sb("cmp_emb", [90, 1])
        small_lim = sb("small_lim", [SMALL, 2])
        wx = [sb(f"wx{l}", [P, 2, 3, H]) for l in range(2)]
        wa = sb("wa", [P, 2, 3, H])
        wh = [sb(f"wh{l}", [P, 3, 2 * H]) for l in range(2)]
        bih = sb("bih", [P, 2, 3])
        bhh = sb("bhh", [P, 2, 3])
        brz = sb("brz", [P, 2, 3])
        act_T = sb("act_T", [P, V_ACT])
        act_tab = sb("act_tab", [64, 3, 2 * H], BF16)
        emb_s = sb("emb_s", [30, 2, P])
        emb_tab = sb("emb_tab", [90, 2, P], BF16)
        bn1 = sb("bn1", [P, 2, FT])
        bn2 = sb("bn2", [P, 2, MT + 1])
        b1 = sb("b1", [P, MT])
        b2 = sb("b2", [P, 2])
        wout = sb("wout", [P, 2])
        bout = sb("bout", [1, 1])
        prime = sb("prime", [1, 12])
        NCOL = T + NPAST + 5
        ids = sb("ids", [P, NCOL * BT], I32)
        ids_ok = sb("ids_ok", [P, NCOL * BT], I32)
        ids_now = sb("ids_now", [P, 2, 2 * BT], I32)
        other = sb("other", [P, B])
        mv1 = sb("mv1", [P, FT, 2])
        st = sb("st", [P, FT, 2, 6])
        std = sb("std", [P, FT])
        ac = sb("ac", [P, 2, FT])
        tmp = sb("tmp", [P, FT])
        st2 = sb("st2", [P, 2, 2, 6])
        mv2 = sb("mv2", [P, 2, 2])
        fold2 = sb("fold2", [P, 2, 5])
        w2r = sb("w2r", [P, 3, N2])
        w1r = sb("w1r", [P, 2, FT, P])
        with nc.sbuf_tensor("XH", [P, FT, B], F32) as XH:
            pass
        x_lo = sb("x_lo", [P, FT, B], F32R)
        with ExitStack() as gru:
            def gb(name, shape, dt=F32):
                return gru.enter_context(nc.sbuf_tensor(name, shape, dt))

            h = gb("h", [P, C, CW])
            r = gb("r", [P, C, CW])
            z = gb("z", [P, C, CW])
            n = gb("n", [P, C, CW])
            onehot = gb("onehot", [64, 2, B], BF16)
            act_rows = gb("act_rows", [64, 2, B], BF16)
            E = gb("E", [P, 6, BT, P])
            work = gb("work", [P, 14 * B])
        x_hi = sb("x_hi", [P, FT, B], F32R)
        h1 = sb("h1", [P, 2, B])
        w_hi = sb("w_hi", [P, 2, FT, P], F32R)
        w_lo = sb("w_lo", [P, 2, FT, P], F32R)
        xs = work[:, 0:4 * B].rearrange("p (par f b) -> p par f b", par=2, f=2)
        xe = work[:, 4 * B:8 * B].rearrange("p (par f b) -> p par f b", par=2, f=2)
        ring = work[:, 8 * B:12 * B].rearrange("p (par f t e) -> p par f t e", par=2, f=2, t=BT)
        t_buf = work[:, 12 * B:13 * B].rearrange("p (c b) -> p c b", c=C)
        zh = work[:, 13 * B:14 * B].rearrange("p (c b) -> p c b", c=C)
        small_i = w1r[0:SMALL, 0, 0:8, :].rearrange("p a b -> p (a b)").bitcast(I32)
        small_f = XH[0:SMALL, 0, :]
        small_g = XH[0:SMALL, 1, :]
        small_b = XH[0:SMALL, 2, 0:B // 2].bitcast(BF16)
        ids_neg = XH[:, 3, 0:NCOL * BT]
        part_rest = XH[0:V_ACT, 4, 0:2 * 6 * H].rearrange("p (k n) -> p k n", k=2)
        part = XH[0:V_ACT, 5, 0:3 * 6 * H // 2].bitcast(BF16).rearrange("p (k n) -> p k n", k=3)
        emb_rest = XH[0:30, 9, 0:2 * 2 * P].rearrange("p (k e n) -> p k e n", k=2, e=2)
        emb_part = XH[0:30, 10, 0:3 * P].bitcast(BF16).rearrange("p (k e n) -> p k e n", k=3, e=2)
        feat_rows = XH[0:90, 6:8, :].rearrange("p a b -> p (a b)").bitcast(BF16).rearrange("p (k b) -> p k b", k=4)
        feat_oh = XH[0:90, 12:14, :].rearrange("p a b -> p (a b)").bitcast(BF16).rearrange("p (k b) -> p k b", k=4)
        sq = work[:, 0:B]
        srow = work[0:1, B:4 * B].rearrange("p (k b) -> p k b", k=3)
        s_sb = work[0:1, 4 * B:5 * B]
        h2 = h1
        y = other[0:1, :]

        ps = ctx.enter_context(nc.psum_tensor("ps", [P, 8, CW], F32))
        ps_r, ps_z, ps_xn = ps[:, 0:2, :], ps[:, 2:4, :], ps[:, 4:6, :]
        ps_hn, ps_t = ps[:, 6, :], ps[:, 7, :]

        s_pre_w = sem("weights_loaded")
        s_ids = sem("ids_loaded")
        s_idok = sem("ids_clamped")
        s_small = sem("small_ids_stored")
        s_dve = sem("dve_setup")
        s_parts = sem("act_table_parts_placed")
        s_tabps = sem("act_table_product")
        s_now = sem("pair_ids_copied")
        s_gath = [sem(f"pair_gathered{i}") for i in range(2)]
        s_fgath = sem("features_gathered")
        s_fring = sem("past_column_gathered")
        s_fpool = sem("past_column_pooled")
        s_fnow = sem("past_ids_copied")
        s_t = sem("quarter_transposed")
        s_ev = sem("quarter_evacuated")
        s_xd = [sem(f"pair_x_stored{i}") for i in range(2)]
        s_xs = [sem(f"step_x_loaded{i}") for i in range(2)]
        s_ar = [sem(f"step_actions_loaded{i}") for i in range(2)]
        s_oh = sem("onehot_built")
        s_px = sem("input_products_done")
        s_pr, s_phn, s_pz = sem("r_product"), sem("hn_product"), sem("z_product")
        s_r, s_z, s_n = sem("r_gate"), sem("z_gate"), sem("n_gate")
        s_t1, s_t2, s_zh, s_zc, s_m, s_h = (sem("r_times_hn"), sem("n_argument"), sem("z_times_h"),
                                            sem("banks_free"), sem("n_part"), sem("h_new"))
        s_hs = [sem(f"h_stored{c}") for c in range(C)]
        s_max = sem("session_max")
        s_ft, s_fe = sem("feature_product"), sem("feature_evacuated")
        s_frow = sem("feature_rows_loaded")
        s_foh = sem("feature_onehots")
        s_fx = sem("feature_vector_ops")
        s_sq = sem("feature_square")
        s_sqp = sem("feature_square_summed")
        s_sum = sem("row_sums")
        s_oth = sem("other_rows")
        s_oth2 = sem("other_sums_placed")
        s_c2 = sem("cont_squared")
        s_sqrt = sem("deviation")
        s_app = sem("features_normalised")
        s_w1 = [sem(f"w1_loaded{i}") for i in range(2)]
        s_hi, s_lo = sem("w1_high_part"), sem("w1_low_part")
        s_xhi = sem("x_high_part")
        s_m1 = sem("dense1_product")
        s_m1e = sem("dense1_relu")
        s_bn = sem("second_norm_step")
        s_dev = sem("second_deviation")
        s_norm = sem("tile_normalised")
        s_w2 = [sem(f"w2_loaded{i}") for i in range(3)]
        s_m2 = sem("dense2_product")
        s_m2e = sem("dense2_relu")
        s_y = sem("logit")
        s_ye = sem("output_ready")
        s_out = sem("output_stored")
        s_tick_pool, s_tick_sp = sem("tick_pool"), sem("tick_sp")
        s_tick_act, s_tick_dve = sem("tick_act"), sem("tick_dve")

        N_W = 19
        L1N = 2 * T

        def col(j):
            return ids_ok[:, j * BT:(j + 1) * BT]

        block = ctx.enter_context(nc.Block())

        @block.sync
        def _(sp):
            sp.dma_start(ids[:], d["ids"]).then_inc(s_ids, 16)
            sp.dma_start(small_i, d["small"]).then_inc(s_ids, 16)
            sp.dma_start(small_lim[:], d["small_lim"]).then_inc(s_ids, 16)
            for dst, src in ((ident[:], d["ident"]), (cmp_act[:], d["cmp_act"]), (cmp_emb[:], d["cmp_emb"]),
                             (wx[0][:], d["wih0"][0:P]), (wa[:], d["wih0"][P:2 * P]), (wx[1][:], d["wih1"]),
                             (bih[:], d["bih"]), (bhh[:], d["bhh"]), (act_T[:], d["act_T"]),
                             (emb_s[:, 0, :], d["emb_price"]), (emb_s[:, 1, :], d["emb_imp"]),
                             (bn1[:], d["bn1"]), (bn2[:], d["bn2"]), (b1[:], d["b1"]), (b2[:], d["b2"])):
                sp.dma_start(dst, src).then_inc(s_pre_w, 16)
            sp.wait_ge(s_dve, 1)
            for l in range(2):
                for f in range(2):
                    sp.dma_start(wh[l][f * H:(f + 1) * H, :, f * H:(f + 1) * H], d[f"whh{l}"][f]).then_inc(s_pre_w, 16)
            sp.wait_ge(s_idok, 4)
            sp.dma_start(small_dram, small_b).then_inc(s_small, 16)
            sp.wait_ge(s_tabps, 2)
            for k in range(3):
                for f in range(2):
                    sp.dma_start(act_tab[32 * f + 10 * k:32 * f + 10 * k + 10, :, f * H:(f + 1) * H],
                                 part[:, k, :].rearrange("p (f g n) -> p f g n", f=2, g=3)[:, f]).then_inc(s_parts, 16)
                sp.dma_start(emb_tab[30 * k:30 * k + 30, :, :], emb_part[:, k, :, :]).then_inc(s_parts, 16)

            def load_x(S, par):
                sp.dma_start(xs[:, par, 0, :], xT_dram[S]).then_inc(s_xs[par], 16)
                sp.dma_start(xs[:, par, 1, :], xT_dram[T - 1 - S]).then_inc(s_xs[par], 16)

            def load_actions(S, par):
                sp.dma_start(act_rows[0:32, par, :], small_dram[S].partition_broadcast(32)).then_inc(s_ar[par], 16)
                sp.dma_start(act_rows[32:64, par, :], small_dram[T - 1 - S].partition_broadcast(32)).then_inc(s_ar[par], 16)

            def load1(S, par):
                sp.dma_start(xs[:, par, 0, :], h0_dram[S]).then_inc(s_xs[par], 16)
                sp.dma_start(xs[:, par, 1, :], h0_dram[T - 1 - S]).then_inc(s_xs[par], 16)

            def store_h(S):
                for c in range(C):
                    sp.wait_ge(s_h, 2 * S + c + 3)
                    sp.dma_start(h0_dram[S, 0:H, c * CW:(c + 1) * CW], h[0:H, c, :]).then_inc(s_hs[c], 16)
                    sp.dma_start(h0_dram[T - 1 - S, H:P, c * CW:(c + 1) * CW], h[H:P, c, :]).then_inc(s_hs[c], 16)

            sp.wait_ge(s_small, 16)
            load_actions(0, 0)
            sp.wait_ge(s_xd[0], 33)
            load_x(0, 0)
            with sp.Fori(0, (T // 2 - PEEL) // 2) as i:
                for u in range(2):
                    S = i * 2 + u
                    sp.wait_ge(s_px, S * 2 + 2)
                    sp.sem_inc(s_tick_sp, 1)
                    sp.wait_ge(s_oh, S + 1)
                    load_actions(S + 1, (u + 1) % 2)
                    sp.wait_ge(s_xd[(u + 1) % 2], (i + (u + 1) // 2) * 32 + 33)
                    load_x(S + 1, (u + 1) % 2)
                    store_h(S)
            sp.wait_ge(s_xd[0], 32 * 8 + 1)
            sp.wait_ge(s_xd[1], 32 * 7 + 1)
            with sp.Fori((T // 2 - PEEL) // 2, T // 2 - 1) as i:
                for u in range(2):
                    S = i * 2 + u
                    sp.wait_ge(s_px, S * 2 + 2)
                    sp.sem_inc(s_tick_sp, 1)
                    sp.wait_ge(s_oh, S + 1)
                    load_actions(S + 1, (u + 1) % 2)
                    load_x(S + 1, (u + 1) % 2)
                    store_h(S)
            sp.wait_ge(s_px, 2 * (T - 2) + 2)
            sp.wait_ge(s_oh, T - 1)
            load_actions(T - 1, 1)
            load_x(T - 1, 1)
            store_h(T - 2)
            sp.wait_ge(s_px, 2 * (T - 1) + 2)
            store_h(T - 1)
            for c in range(C):
                sp.wait_ge(s_hs[c], 32 * T + 1)
            load1(0, 0)
            with sp.Fori(0, T // 2 - 1) as i:
                for u in range(2):
                    S = i * 2 + u
                    sp.wait_ge(s_px, S * 2 + 2 + L1N)
                    load1(S + 1, (u + 1) % 2)
            sp.wait_ge(s_px, 2 * (T - 2) + 2 + L1N)
            load1(T - 1, 1)
            for k in range(4):
                sp.dma_start(feat_rows[:, k, :], small_dram[T + k].partition_broadcast(90)).then_inc(s_frow, 16)
            sp.wait_ge(s_c2, 1)
            sp.dma_start(other[R_CONT:R_CONT + N_CONT, :], d["cont_T"]).then_inc(s_oth, 16)
            sp.dma_start(other[R_NEIGH:R_NEIGH + N_NEIGH, :], d["neigh_T"]).then_inc(s_oth, 16)
            sp.dma_start(wout[:], d["wout"]).then_inc(s_oth, 16)
            sp.dma_start(bout[:], d["bout"]).then_inc(s_oth, 16)
            for m in range(2):
                sp.dma_start(w1r[:, m], d["w1"][m]).then_inc(s_w1[m], 16)
            sp.wait_ge(s_sum, 2)
            for k, row in enumerate((R_SUM2, R_SQ, R_SECOND)):
                sp.dma_start(other[row:row + 1, :], srow[:, k, :]).then_inc(s_oth2, 16)
            sp.dma_start(w2r[:, 2], d["w2"][:, MT]).then_inc(s_w2[2], 16)
            for m in range(2):
                sp.dma_start(w2r[:, m], d["w2"][:, m]).then_inc(s_w2[m], 16)
            with sp.Fori(0, MT // 2) as i:
                for u in range(2):
                    m = i * 2 + u
                    sp.wait_ge(s_lo, m + 1)
                    sp.dma_start(w1r[:, u], d["w1"][m + 2]).then_inc(s_w1[u], 16)
                    sp.wait_ge(s_m2, m + 2)
                    sp.dma_start(w2r[:, u], d["w2"][:, m + 2]).then_inc(s_w2[u], 16)
            sp.wait_ge(s_w2[1], 16 * (MT // 2 + 1))
            sp.wait_ge(s_ye, 1)
            sp.dma_start(out, y).then_inc(s_out, 16)
            sp.wait_ge(s_out, 16)

        @block.gpsimd
        def _(pool):
            pool.wait_ge(s_idok, 3)

            def gather(dst, idx, table, done):
                pool.indirect_dma_start(dst, None, table,
                                        bass.IndirectOffsetOnAxis(ap=idx.bitcast(U32), axis=0)).then_inc(done, 16)

            def gather_pair(j, par, first=False):
                nc.gpsimd.tensor_copy(ids_now[:, par, :], ids_ok[:, bass.ds(j * (2 * BT), 2 * BT)]).then_inc(s_now, 1)
                pool.wait_ge(s_now, j + 1)
                pool.sem_inc(s_tick_pool, 1)
                for f in range(2):
                    for b in range(BT):
                        gather(ring[:, par, f, b, :], ids_now[:, par, f * BT + b:f * BT + b + 1], d["emb_item"],
                               s_gath[par])

            gather_pair(0, 0)
            gather_pair(1, 1)
            with pool.Fori(1, PAIRS // 2) as i:
                for u in range(2):
                    j = i * 2 + u
                    pool.wait_ge(s_t, (j - 1) * 4)
                    gather_pair(j, u)
            pool.wait_ge(s_t, (PAIRS - 2) * 4)
            gather_pair(PAIRS - 1, 0)
            at = T + NPAST
            for slot, table in ((G_ITEM, "emb_item"), (G_LAST, "emb_item"), (G_LCI, "emb_item"),
                                (G_CITY, "emb_city"), (G_CP, "emb_cp")):
                for b in range(BT):
                    gather(E[:, slot, b, :], col(at + slot)[:, b:b + 1], d[table], s_fgath)
            for b in range(BT):
                gather(E[:, G_POOL, b, :], col(T)[:, b:b + 1], d["emb_item"], s_fring)
            pool.wait_ge(s_t, PAIRS * 4)
            with pool.Fori(1, NPAST) as k:
                pool.wait_ge(s_fpool, k)
                nc.gpsimd.tensor_copy(ids_now[:, 1, 0:BT], ids_ok[:, bass.ds((k + T) * BT, BT)]).then_inc(s_fnow, 1)
                pool.wait_ge(s_fnow, k)
                pool.sem_inc(s_tick_pool, 1)
                for b in range(BT):
                    gather(ring[:, 1, 0, b, :], ids_now[:, 1, b:b + 1], d["emb_item"], s_fring)

        @block.tensor
        def _(pe):
            pe.wait_ge(s_pre_w, 16 * N_W)
            pe.wait_ge(s_dve, 5)
            nc.tensor.matmul(ps_hn[0:V_ACT, 0:384], act_T[:], wa[:].rearrange("p f g n -> p (f g n)"),
                             start=True, stop=True).then_inc(s_tabps, 1)

            def transpose_quarter(q, par, w_gath, w_ev):
                if q == 0:
                    pe.wait_ge(s_gath[par], w_gath)
                pe.wait_ge(s_ev, w_ev)
                f, half = q // 2, q % 2
                for k in range(4):
                    last = nc.tensor.transpose(ps_t[:, k * P:(k + 1) * P], ring[:, par, f, 4 * half + k, :], ident[:])
                last.then_inc(s_t, 1)

            def x_product(l, c, par, N):
                pe.wait_ge(s_zc, N + 1)
                for g, bank in enumerate((ps_r, ps_z, ps_xn)):
                    for f in range(2):
                        last = nc.tensor.matmul(bank[f * H:(f + 1) * H, c, :], wx[l][:, f, g, :],
                                                xs[:, par, f, c * CW:(c + 1) * CW], start=True,
                                                stop=(l == 1 and g == 2), skip_group_check=True)
                if l == 0:
                    for g, bank in enumerate((ps_r, ps_z, ps_xn)):
                        last = nc.tensor.matmul(bank[:, c, :], act_tab[:, g, :],
                                                onehot[:, par, c * CW:(c + 1) * CW], start=False, stop=(g == 2),
                                                skip_group_check=True)
                last.then_inc(s_px, 1)

            def h_product(l, c, N):
                pe.wait_ge(s_h, N + 1 + 2 * l)
                nc.tensor.matmul(ps_r[:, c, :], wh[l][:, 0, :], h[:, c, :], start=False, stop=True,
                                 skip_group_check=True).then_inc(s_pr, 1)
                pe.wait_ge(s_t1, N + 1)
                nc.tensor.matmul(ps_hn, wh[l][:, 2, :], h[:, c, :], start=True, stop=True).then_inc(s_phn, 1)
                nc.tensor.matmul(ps_z[:, c, :], wh[l][:, 1, :], h[:, c, :], start=False, stop=True,
                                 skip_group_check=True).then_inc(s_pz, 1)

            for j in range(PEEL):
                for q in range(4):
                    transpose_quarter(q, j % 2, 256 * (j // 2 + 1), 4 * j + q + 1)
            pe.wait_ge(s_parts, 16 * 9)
            with pe.Fori(0, (T // 2 - PEEL) // 2) as i:
                for u in range(2):
                    S = i * 2 + u
                    j, jp = S + PEEL, (u + PEEL) % 2
                    wg = (i + (u + PEEL) // 2 + 1) * 256
                    pe.wait_ge(s_xs[u], (i + 1) * 32)
                    pe.wait_ge(s_oh, S + 1)
                    x_product(0, 0, u, S * 2)
                    transpose_quarter(0, jp, wg, j * 4 + 1)
                    h_product(0, 0, S * 2)
                    transpose_quarter(1, jp, wg, j * 4 + 2)
                    x_product(0, 1, u, S * 2 + 1)
                    transpose_quarter(2, jp, wg, j * 4 + 3)
                    h_product(0, 1, S * 2 + 1)
                    transpose_quarter(3, jp, wg, j * 4 + 4)
            with pe.Fori((T // 2 - PEEL) // 2, T // 2) as i:
                for u in range(2):
                    S = i * 2 + u
                    pe.wait_ge(s_xs[u], (i + 1) * 32)
                    pe.wait_ge(s_oh, S + 1)
                    for c in range(C):
                        x_product(0, c, u, S * 2 + c)
                        h_product(0, c, S * 2 + c)
            with pe.Fori(T // 2, T) as i:
                for u in range(2):
                    S = i * 2 + u
                    pe.wait_ge(s_xs[u], (i + 1) * 32)
                    for c in range(C):
                        x_product(1, c, u, S * 2 + c)
                        h_product(1, c, S * 2 + c)

            pe.wait_ge(s_fgath, 16 * BT * 5)
            pe.wait_ge(s_fpool, NPAST)
            pe.wait_ge(s_max, 2 * T + 2)
            for k, (slot, x) in enumerate(FEATURES):
                if k >= 4:
                    pe.wait_ge(s_fe, k - 3)
                bk = 2 * (k % 4)
                for half in range(2):
                    bank = ps[:, bk + half, :]
                    if k < 6:
                        for q in range(4):
                            last = nc.tensor.transpose(bank[:, q * P:(q + 1) * P], E[:, slot, 4 * half + q, :], ident[:])
                    else:
                        if k == 6:
                            pe.wait_ge(s_foh, 1)
                        last = nc.tensor.matmul(bank, emb_tab[:, slot, :], feat_oh[:, k - 6, half * CW:(half + 1) * CW],
                                                start=True, stop=True)
                last.then_inc(s_ft, 1)
            pe.wait_ge(s_fe, 10)
            for k in range(6):
                for half in range(2):
                    last = nc.tensor.matmul(ps[0:1, half, :], ones[:], XH[:, k, half * CW:(half + 1) * CW],
                                            start=(k == 0), stop=(k == 5))
            for k in range(6):
                pe.wait_ge(s_sq, k + 1)
                for half in range(2):
                    last = nc.tensor.matmul(ps[0:1, 2 + half, :], ones[:], sq[:, half * CW:(half + 1) * CW],
                                            start=(k == 0), stop=(k == 5))
                last.then_inc(s_sqp, 1)

            def dense1(m, par, w_m1e):
                pe.wait_ge(s_lo, m + 1)
                pe.wait_ge(s_m1e, w_m1e)
                for half in range(2):
                    bank = ps[:, 4 + 2 * par + half, :]
                    cols = slice(half * CW, (half + 1) * CW)
                    for k in range(FT):
                        if isinstance(m, int) and m == 0 and half == 0:
                            pe.wait_ge(s_app, k + 1)
                        nc.tensor.matmul(bank, w_lo[:, par, k, :], x_hi[:, k, cols], start=(k == 0), stop=False)
                        nc.tensor.matmul(bank, w_hi[:, par, k, :], x_lo[:, k, cols], start=False, stop=False)
                        last = nc.tensor.matmul(bank, w_hi[:, par, k, :], x_hi[:, k, cols], start=False,
                                                stop=(k == FT - 1))
                    last.then_inc(s_m1, 1)

            def dense2(w_norm, slot, w_w2, rhs, start=False, stop=False):
                pe.wait_ge(s_norm, w_norm)
                pe.wait_ge(s_w2[slot], w_w2)
                for m2 in range(2):
                    for half in range(2):
                        last = nc.tensor.matmul(ps[:, 2 * m2 + half, :], w2r[:, slot, m2 * P:(m2 + 1) * P],
                                                rhs[:, half * CW:(half + 1) * CW], start=start, stop=stop,
                                                skip_group_check=True)
                last.then_inc(s_m2, 1)

            dense1(0, 0, 2)
            dense2(1, 2, 16, other, start=True)
            with pe.Fori(0, MT // 2) as i:
                for u in range(2):
                    m = i * 2 + u
                    dense1(m + 1, 1 - u, m * 2 + 2)
                    dense2(m + 2, u, (i + 1) * 16, h1[:, u, :])
            dense2(MT + 1, 0, 16 * (MT // 2 + 1), h1[:, 0, :], stop=True)
            pe.wait_ge(s_m2e, 4)
            for half in range(2):
                for m in range(2):
                    last = nc.tensor.matmul(ps[0:1, 4 + half, :], wout[:, m:m + 1], h2[:, m, half * CW:(half + 1) * CW],
                                            start=(m == 0), stop=(m == 1))
            last.then_inc(s_y, 1)

        @block.scalar
        def _(act):
            act.wait_ge(s_pre_w, 16 * N_W)
            act.wait_ge(s_dve, 5)

            def evacuate(j, q, par):
                act.wait_ge(s_t, j * 4 + q + 1)
                nc.scalar.activation(xe[:, par, q // 2, (q % 2) * CW:(q % 2 + 1) * CW], ps_t, ACT.Copy).then_inc(s_ev, 1)

            def store_pair(j, par):
                act.wait_ge(s_ev, j * 4 + 5)
                act.dma_start(xT_dram[j], xe[:, par, 0, :]).then_inc(s_xd[par], 16)
                act.dma_start(xT_dram[T - 1 - j], xe[:, par, 1, :]).then_inc(s_xd[par], 16)

            def gates(l, c, N):
                act.wait_ge(s_pr, N + 1)
                nc.scalar.activation(r[:, c, :], ps_r[:, c, :], ACT.Sigmoid, bias=brz[:, l, 0:1]).then_inc(s_r, 1)
                act.wait_ge(s_pz, N + 1)
                nc.scalar.activation(z[:, c, :], ps_z[:, c, :], ACT.Sigmoid, bias=brz[:, l, 1:2]).then_inc(s_z, 1)

            def new(l, c, N):
                act.wait_ge(s_t2, N + 1)
                nc.scalar.activation(n[:, c, :], t_buf[:, c, :], ACT.Tanh, bias=bih[:, l, 2:3]).then_inc(s_n, 1)

            for j in range(PEEL):
                if j >= 2:
                    act.wait_ge(s_xd[j % 2], 32 * (j // 2) + 1)
                for q in range(4):
                    evacuate(j, q, j % 2)
                store_pair(j, j % 2)
            with act.Fori(0, (T // 2 - PEEL) // 2) as i:
                for u in range(2):
                    S = i * 2 + u
                    j, jp = S + PEEL, (u + PEEL) % 2
                    act.wait_ge(s_xd[jp], (i + (u + PEEL) // 2) * 32 + 1)
                    evacuate(j, 0, jp)
                    gates(0, 0, S * 2)
                    evacuate(j, 1, jp)
                    new(0, 0, S * 2)
                    evacuate(j, 2, jp)
                    gates(0, 1, S * 2 + 1)
                    evacuate(j, 3, jp)
                    store_pair(j, jp)
                    new(0, 1, S * 2 + 1)
            for l, first, end in ((0, (T // 2 - PEEL) // 2, T // 2), (1, T // 2, T)):
                with act.Fori(first, end) as i:
                    for u in range(2):
                        for c in range(C):
                            gates(l, c, i * 4 + 2 * u + c)
                            new(l, c, i * 4 + 2 * u + c)

            for k, (slot, x) in enumerate(FEATURES):
                act.wait_ge(s_ft, k + 1)
                bk = 2 * (k % 4)
                nc.scalar.activation(XH[:, x, :], ps[:, bk:bk + 2, :].rearrange("p a b -> p (a b)"), ACT.Copy)\
                    .then_inc(s_fe, 1)
            act.wait_ge(s_fe, 10)
            for k in range(6):
                if k:
                    act.wait_ge(s_sqp, k)
                nc.scalar.activation(sq, XH[:, k, :], ACT.Square).then_inc(s_sq, 1)
            act.wait_ge(s_oth, 64)
            nc.scalar.activation(other[R_CONT2:R_CONT2 + N_CONT, :], other[R_CONT:R_CONT + N_CONT, :], ACT.Square)\
                .then_inc(s_c2, 1)
            act.wait_ge(s_fx, 6)
            nc.scalar.activation(tmp[:, 0:FT], tmp[:, 0:FT], ACT.Sqrt).then_inc(s_sqrt, 1)
            act.wait_ge(s_fx, 10)
            act.wait_ge(s_oth2, 48)

            def split_hi(m, par, w_w1, w_m1):
                act.wait_ge(s_w1[par], w_w1)
                if w_m1 is not None:
                    act.wait_ge(s_m1, w_m1)
                nc.scalar.activation(w_hi[:, par], w1r[:, par], ACT.Copy).then_inc(s_hi, 1)

            split_hi(0, 0, 16, None)
            for k in range(FT):
                nc.scalar.activation(XH[:, k, :], XH[:, k, :], ACT.Identity, bias=std[:, k:k + 1],
                                     scale=ac[:, 0, k:k + 1]).then_inc(s_xhi, 1)
                act.wait_ge(s_xhi, 2 * k + 1)
                nc.scalar.activation(x_hi[:, k, :], XH[:, k, :], ACT.Copy).then_inc(s_xhi, 1)
            split_hi(1, 1, 16, None)

            def deviation(par, w_bn):
                act.wait_ge(s_bn, w_bn)
                nc.scalar.activation(fold2[:, par, 0:1], fold2[:, par, 0:1], ACT.Sqrt).then_inc(s_dev, 1)

            def relu1(m, par):
                act.wait_ge(s_m2, m)
                for half in range(2):
                    act.wait_ge(s_m1, m * 2 + half + 1)
                    act.sem_inc(s_tick_act, 1)
                    nc.scalar.activation(h1[:, par, half * CW:(half + 1) * CW], ps[:, 4 + 2 * par + half, :], ACT.Relu,
                                         bias=b1[:, bass.ds(m, 1)]).then_inc(s_m1e, 1)
                deviation(par, m * 7 + 10)

            deviation(0, 3)
            with act.Fori(0, MT // 2) as i:
                for u in range(2):
                    m = i * 2 + u
                    relu1(m, u)
                    split_hi(m + 2, u, (i + 2) * 16, m * 2 + 2)
            relu1(MT - 1, 0)
            act.wait_ge(s_m2, MT + 1)
            for m in range(2):
                for half in range(2):
                    nc.scalar.activation(h2[:, m, half * CW:(half + 1) * CW], ps[:, 2 * m + half, :], ACT.Relu,
                                         bias=b2[:, m:m + 1]).then_inc(s_m2e, 1)
            act.wait_ge(s_y, 1)
            nc.scalar.activation(y, ps[0:1, 4:6, :].rearrange("p a b -> p (a b)"), ACT.Sigmoid, bias=bout[:])\
                .then_inc(s_ye, 1)

        @block.vector
        def _(dve):
            V = nc.vector
            for l in range(2):
                last = V.memset(wh[l][:], 0.0)
            last.then_inc(s_dve, 1)
            V.memset(act_tab[:], 0.0)
            V.memset(ones[:], 1.0)
            V.memset(h[:], 0.0).then_inc(s_h, 2)
            V.memset(prime[:, 0:1], 0.0).then_inc(s_zc, 2)
            V.memset(prime[:, 1:2], 0.0).then_inc(s_t1, 1)
            V.memset(prime[:, 2:3], 0.0).then_inc(s_ev, 1)
            for c in range(C):
                V.memset(prime[:, 6 + c:7 + c], 0.0).then_inc(s_hs[c], 1)
                V.memset(prime[:, 10 + c:11 + c], 0.0).then_inc(s_m1e, 1)
                V.memset(prime[:, 8 + c:9 + c], 0.0).then_inc(s_xd[c], 1)
            V.memset(prime[:, 5:6], 0.0).then_inc(s_fpool, 1)
            V.memset(prime[:, 3:4], 0.0).then_inc(s_px, 2)
            V.memset(XH[:, X_SESS, :], -3.0e38).then_inc(s_max, 2)
            dve.wait_ge(s_ids, 48)
            n_item = (T + NPAST + 3) * BT
            ranges = ((0, n_item, V_ITEM), (n_item, n_item + BT, V_CITY), (n_item + BT, n_item + 2 * BT, V_CP))
            for a, b, v in ranges:
                last = V.tensor_scalar(ids_neg[:, a:b], ids[:, a:b], 0.0, float(v), ALU.is_lt, ALU.mult)
            V.tensor_scalar(small_f, small_i, 0.0, small_lim[:, 0:1], ALU.is_lt, ALU.mult).then_inc(s_idok, 1)
            dve.wait_ge(s_idok, 1)
            V.tensor_tensor(ids_neg, ids[:], ids_neg, ALU.add)
            V.tensor_tensor(small_g, small_i, small_f, ALU.add).then_inc(s_idok, 1)
            dve.wait_ge(s_idok, 2)
            for a, b, v in ranges:
                last = V.tensor_scalar(ids_ok[:, a:b], ids_neg[:, a:b], 0.0, float(v - 1), ALU.max, ALU.min)
            last.then_inc(s_idok, 1)
            V.tensor_scalar(small_b, small_g, 0.0, small_lim[:, 1:2], ALU.max, ALU.min).then_inc(s_idok, 1)
            dve.wait_ge(s_pre_w, 16 * N_W)
            V.tensor_tensor(brz[:], bih[:], bhh[:], ALU.add).then_inc(s_dve, 4)
            dve.wait_ge(s_tabps, 1)
            count = [5]

            def link(ins):
                ins.then_inc(s_dve, 1)
                count[0] += 1
                dve.wait_ge(s_dve, count[0])

            for parts, rest, src in ((part, part_rest, ps_hn[0:V_ACT, 0:384]), (emb_part, emb_rest, emb_s[:])):
                link(V.tensor_copy(parts[:, 0], src))
                link(V.tensor_tensor(rest[:, 0], src, parts[:, 0], ALU.subtract))
                link(V.tensor_copy(parts[:, 1], rest[:, 0]))
                link(V.tensor_tensor(rest[:, 1], rest[:, 0], parts[:, 1], ALU.subtract))
                link(V.tensor_copy(parts[:, 2], rest[:, 1]))
            V.memset(prime[:, 4:5], 0.0).then_inc(s_tabps, 1)

            def build_onehot(S, par, w_rows):
                dve.wait_ge(s_ar[par], w_rows)
                dve.wait_ge(s_px, S * 2)
                V.tensor_scalar(onehot[:, par, :], act_rows[:, par, :], cmp_act[:], None, ALU.is_equal).then_inc(s_oh, 1)

            def cell(l, c, N, w_store):
                dve.wait_ge(s_r, N + 1)
                dve.wait_ge(s_phn, N + 1)
                V.scalar_tensor_tensor(t_buf[:, c, :], ps_hn, bhh[:, l, 2:3], r[:, c, :], ALU.add, ALU.mult)\
                    .then_inc(s_t1, 1)
                dve.wait_ge(s_t1, N + 2)
                V.tensor_tensor(t_buf[:, c, :], t_buf[:, c, :], ps_xn[:, c, :], ALU.add).then_inc(s_t2, 1)
                dve.wait_ge(s_z, N + 1)
                V.tensor_tensor(zh[:, c, :], z[:, c, :], h[:, c, :], ALU.mult).then_inc(s_zh, 1)
                dve.wait_ge(s_zh, N + 1)
                V.tensor_scalar(z[:, c, :], z[:, c, :], -1.0, 1.0, ALU.mult, ALU.add).then_inc(s_zc, 1)
                dve.wait_ge(s_zc, N + 3)
                dve.wait_ge(s_n, N + 1)
                V.tensor_tensor(n[:, c, :], n[:, c, :], z[:, c, :], ALU.mult).then_inc(s_m, 1)
                dve.wait_ge(s_m, N + 1)
                if w_store is not None:
                    dve.wait_ge(s_hs[c], w_store)
                V.tensor_tensor(h[:, c, :], n[:, c, :], zh[:, c, :], ALU.add).then_inc(s_h, 1)

            build_onehot(0, 0, 32)
            with dve.Fori(0, T // 2 - 1) as i:
                for u in range(2):
                    S = i * 2 + u
                    cell(0, 0, S * 2, S * 32 + 1)
                    build_onehot(S + 1, (u + 1) % 2, (i + (u + 1) // 2 + 1) * 32)
                    cell(0, 1, S * 2 + 1, S * 32 + 1)
            cell(0, 0, 2 * (T - 2), 32 * (T - 2) + 1)
            build_onehot(T - 1, 1, 32 * (T // 2))
            cell(0, 1, 2 * (T - 2) + 1, 32 * (T - 2) + 1)
            for c in range(C):
                cell(0, c, 2 * (T - 1) + c, 32 * (T - 1) + 1)
            for c in range(C):
                dve.wait_ge(s_hs[c], 32 * T + 1)
            V.memset(h[:], 0.0).then_inc(s_h, 2)

            def cell_max(c, N):
                cell(1, c, N, None)
                dve.wait_ge(s_h, N + 5)
                dve.wait_ge(s_max, N - (2 * T - 2))
                V.tensor_tensor(XH[:, X_SESS, c * CW:(c + 1) * CW], XH[:, X_SESS, c * CW:(c + 1) * CW],
                                h[:, c, :], ALU.max).then_inc(s_max, 1)

            with dve.Fori(T // 2, T // 2 + NPAST - 1) as i:
                for u in range(2):
                    for c in range(C):
                        cell_max(c, i * 4 + 2 * u + c)
                dve.wait_ge(s_fring, (i - (T // 2 - 2)) * (16 * BT))
                dve.wait_ge(s_fpool, i - (T // 2 - 1))
                V.tensor_tensor(E[:, G_POOL], E[:, G_POOL], ring[:, 1, 0], ALU.max).then_inc(s_fpool, 1)
            with dve.Fori(T // 2 + NPAST - 1, T) as i:
                for u in range(2):
                    for c in range(C):
                        cell_max(c, i * 4 + 2 * u + c)

            V.memset(other[:], 0.0).then_inc(s_c2, 1)
            dve.wait_ge(s_frow, 64)
            V.tensor_scalar(feat_oh[:, :, :], feat_rows[:, :, :], cmp_emb[:], None, ALU.is_equal).then_inc(s_foh, 1)
            dve.wait_ge(s_fe, 10)
            dve.wait_ge(s_foh, 1)
            for o, a, b in ((X_INTER, X_ITEM, X_POOL), (X_ILAST, X_ITEM, X_LAST), (X_ILC, X_ITEM, X_LCI),
                            (X_IMPL, X_IMP, X_LII)):
                last = V.tensor_tensor(XH[:, o, :], XH[:, a, :], XH[:, b, :], ALU.mult)
            last.then_inc(s_fx, 1)
            dve.wait_ge(s_sqp, 6)
            V.tensor_copy(s_sb, ps[0:1, 0:2, :].rearrange("p a b -> p (a b)"))
            V.tensor_copy(srow[:, 1, :], ps[0:1, 2:4, :].rearrange("p a b -> p (a b)")).then_inc(s_sum, 1)
            dve.wait_ge(s_sum, 1)
            V.tensor_tensor(srow[:, 0, :], s_sb, s_sb, ALU.mult).then_inc(s_fx, 1)
            dve.wait_ge(s_fx, 2)
            V.tensor_tensor(srow[:, 2, :], srow[:, 0, :], srow[:, 1, :], ALU.subtract).then_inc(s_fx, 1)
            dve.wait_ge(s_fx, 3)
            V.tensor_scalar(srow[:, 2, :], srow[:, 2, :], 0.5, None, ALU.mult).then_inc(s_sum, 1)

            def stats(src, k):
                for half in range(2):
                    last = V.bn_stats(st[:, k, half, :], src[:, half * CW:(half + 1) * CW])
                return last

            def fold(mv, bn, count, w):
                V.tensor_scalar(tmp[:, 0:count], mv[:, 0:count, 1], EPS, None, ALU.add).then_inc(s_fx, 1)
                dve.wait_ge(s_sqrt, 1 if w == 6 else 2)
                V.reciprocal(std[:, 0:count], tmp[:, 0:count]).then_inc(s_fx, 1)
                dve.wait_ge(s_fx, w + 1)
                V.tensor_tensor(ac[:, 0, 0:count], std[:, 0:count], bn[:, 0, 0:count], ALU.mult).then_inc(s_fx, 1)
                dve.wait_ge(s_fx, w + 2)
                V.tensor_tensor(ac[:, 1, 0:count], ac[:, 0, 0:count], mv[:, 0:count, 0], ALU.mult).then_inc(s_fx, 1)
                dve.wait_ge(s_fx, w + 3)
                V.tensor_tensor(std[:, 0:count], bn[:, 1, 0:count], ac[:, 1, 0:count], ALU.subtract).then_inc(s_fx, 1)

            for k in range(FT):
                last = stats(XH[:, k, :], k)
            last.then_inc(s_fx, 1)
            dve.wait_ge(s_fx, 4)
            for k in range(FT):
                last = V.bn_aggr(mv1[:, k, :], st[:, k, :, :].rearrange("p a b -> p (a b)"))
            last.then_inc(s_fx, 1)
            dve.wait_ge(s_fx, 5)
            fold(mv1, bn1, FT, 6)
            def split_lo(m, par, w_m1):
                if w_m1 is not None:
                    dve.wait_ge(s_m1, w_m1)
                dve.wait_ge(s_hi, m + 1)
                V.tensor_tensor(w_lo[:, par], w1r[:, par], w_hi[:, par], ALU.subtract).then_inc(s_lo, 1)

            def normalise(par, m, src, col, at):
                for half in range(2):
                    if m is not None:
                        dve.wait_ge(s_m1e, m * 2 + half + 3)
                    last = V.bn_stats(st2[:, par, half, :], src[:, half * CW:(half + 1) * CW])
                last.then_inc(s_bn, 1)
                dve.wait_ge(s_bn, at + 1)
                dve.sem_inc(s_tick_dve, 1)
                V.bn_aggr(mv2[:, par, :], st2[:, par].rearrange("p a b -> p (a b)")).then_inc(s_bn, 1)
                dve.wait_ge(s_bn, at + 2)
                V.tensor_scalar(fold2[:, par, 0:1], mv2[:, par, 1:2], EPS, None, ALU.add).then_inc(s_bn, 1)
                dve.wait_ge(s_dev, 1 if m is None else m + 2)
                V.reciprocal(fold2[:, par, 1:2], fold2[:, par, 0:1]).then_inc(s_bn, 1)
                dve.wait_ge(s_bn, at + 4)
                V.tensor_tensor(fold2[:, par, 2:3], fold2[:, par, 1:2], bn2[:, 0, col], ALU.mult).then_inc(s_bn, 1)
                dve.wait_ge(s_bn, at + 5)
                V.tensor_tensor(fold2[:, par, 3:4], fold2[:, par, 2:3], mv2[:, par, 0:1], ALU.mult).then_inc(s_bn, 1)
                dve.wait_ge(s_bn, at + 6)
                V.tensor_tensor(fold2[:, par, 4:5], bn2[:, 1, col], fold2[:, par, 3:4], ALU.subtract).then_inc(s_bn, 1)
                dve.wait_ge(s_bn, at + 7)
                V.tensor_scalar(src, src, fold2[:, par, 2:3], fold2[:, par, 4:5], ALU.mult, ALU.add).then_inc(s_norm, 1)

            dve.wait_ge(s_oth2, 48)
            split_lo(0, 0, None)
            for k in range(FT):
                dve.wait_ge(s_xhi, 2 * k + 2)
                V.tensor_tensor(x_lo[:, k, :], XH[:, k, :], x_hi[:, k, :], ALU.subtract).then_inc(s_app, 1)
            split_lo(1, 1, None)
            dve.wait_ge(s_c2, 2)
            normalise(0, None, other[:], slice(MT, MT + 1), 0)
            with dve.Fori(0, MT // 2) as i:
                for u in range(2):
                    m = i * 2 + u
                    normalise(u, m, h1[:, u, :], bass.ds(m, 1), m * 7 + 7)
                    split_lo(m + 2, u, m * 2 + 2)
            normalise(0, MT - 1, h1[:, 0, :], slice(MT - 1, MT), 7 * MT)


FEATURES = ((G_ITEM, X_ITEM), (G_POOL, X_POOL), (G_LAST, X_LAST), (G_LCI, X_LCI), (G_CITY, X_CITY), (G_CP, X_CP),
            (0, X_PRICE), (1, X_IMP), (1, X_LCIMP), (1, X_LII))


def kernel(**a):
    import numpy as np
    import concourse.bacc as bacc
    from concourse import mybir
    from concourse.bass_utils import run_bass_kernel_spmd

    v = {k: np.asarray(x) for k, x in a.items()}

    def w(name):
        return v["L0_rec_" + name]

    def tiles(x):
        x = x.reshape(B, -1)
        return x.reshape(BT, P, -1).transpose(1, 2, 0)

    sess = v["r_past_interactions_sess"]
    order = [t for j in range(PAIRS) for t in (j, T - 1 - j)]
    cols = [tiles(sess[:, order]), tiles(v["r_past_interactions"])]
    cols += [tiles(v[k]) for k in ("r_item_id", "r_last_item", "r_last_click_item", "r_city", "r_city_platform")]
    ids = np.concatenate(cols, axis=1).reshape(P, -1)
    small = np.concatenate([v["r_past_actions_sess"].T] + [v[k][None, :] for k in (
        "r_price_rank", "r_impression_index", "r_last_click_impression", "r_last_interact_index")], axis=0)
    vocab = np.array([V_ACT] * T + [V_PRICE, V_IMP, V_IMP, V_IMP], np.float32)
    row = np.arange(64)

    def wih(x):
        return x.transpose(2, 0, 1).reshape(x.shape[2], 2, 3, H)

    def gates(x0, x1):
        return np.stack([x.reshape(2, 3, H).transpose(0, 2, 1).reshape(P, 3) for x in (x0, x1)], axis=1)

    def other(x, axis):
        x = np.moveaxis(x, axis, 0)
        res = np.zeros((MT * P + P,) + x.shape[1:], x.dtype)
        res[0:H1] = x[N_CONT:N_CONT + H1]
        o = MT * P
        e = N_CONT + H1
        res[o + R_CONT:o + R_CONT + N_CONT] = x[0:N_CONT]
        for k, dst in enumerate((R_SUM2, R_SQ, R_SECOND)):
            res[o + dst] = x[e + k]
        res[o + R_CONT2:o + R_CONT2 + N_CONT] = x[e + 3:e + 3 + N_CONT]
        res[o + R_NEIGH:o + R_NEIGH + N_NEIGH] = x[e + 3 + N_CONT:]
        return res

    w1 = np.zeros(((MT + 1) * P, FT * P), np.float32)
    w1[0:H1] = w("w1")
    b1 = np.zeros((MT * P,), np.float32)
    b1[0:H1] = w("b1")
    arrays = {
        "ids": ids,
        "small": small,
        "small_lim": np.stack([vocab, vocab - 1], axis=1),
        "ident": np.eye(P, dtype=np.float32),
        "cmp_act": np.where(row % 32 < 30, row % 32 % 10, -1).astype(np.float32)[:, None],
        "cmp_emb": (np.arange(90) % 30).astype(np.float32)[:, None],
        "wih0": wih(w("gru_wih0")),
        "wih1": wih(w("gru_wih1")),
        "whh0": wih(w("gru_whh0")).transpose(1, 0, 2, 3),
        "whh1": wih(w("gru_whh1")).transpose(1, 0, 2, 3),
        "bih": gates(w("gru_bih0"), w("gru_bih1")),
        "bhh": gates(w("gru_bhh0"), w("gru_bhh1")),
        "act_T": w("emb_act").T,
        "emb_price": w("emb_price"),
        "emb_imp": w("emb_imp"),
        "emb_item": w("emb_item"),
        "emb_city": w("emb_city"),
        "emb_cp": w("emb_cp"),
        "bn1": np.stack([w("bn_g"), w("bn_b")]).reshape(2, FT, P).transpose(2, 0, 1),
        "bn2": np.stack([other(w("bn_g"), 0), other(w("bn_b"), 0)]).reshape(2, MT + 1, P).transpose(2, 0, 1),
        "w1": w1.reshape(MT + 1, P, FT, P).transpose(0, 3, 2, 1),
        "b1": b1.reshape(MT, P).T,
        "w2": other(w("w2"), 1).reshape(MT + 1, P, N2).transpose(1, 0, 2),
        "b2": w("b2").reshape(2, P).T,
        "wout": w("wout").reshape(2, P).T,
        "bout": w("bout").reshape(1, 1),
        "cont_T": v["r_cont_features"].T,
        "neigh_T": v["r_neighbor_prices"].T,
    }
    arrays = {k: np.ascontiguousarray(x) for k, x in arrays.items()}
    nc = bacc.Bacc("TRN2", target_bir_lowering=False, num_devices=1)
    aps = {k: nc.dram_tensor("in_" + k, x.shape, mybir.dt.from_np(x.dtype), kind="ExternalInput").ap()
           for k, x in arrays.items()}
    out = nc.dram_tensor("out", (1, B), F32, kind="ExternalOutput").ap()
    rec_kernel(nc, aps, out)
    res = run_bass_kernel_spmd(nc, [{"in_" + k: x for k, x in arrays.items()}], core_ids=[0])
    return res.results[0]["out"].reshape(B)
```

```python
from contextlib import ExitStack

import concourse.bass as bass
from concourse import mybir

ALU = mybir.AluOpType
ACT = mybir.ActivationFunctionType
F32 = mybir.dt.float32
F32R = mybir.dt.float32r
BF16 = mybir.dt.bfloat16
I32 = mybir.dt.int32
U32 = mybir.dt.uint32

P = 128
H = 64
T = 30
B = 1024
BT = B // P
C = 2
CW = B // C
PAIRS = T // 2
OWN = PAIRS - 1
FROM_DRAM = PAIRS + 1
NPAST = 10
STATS_END = T // 2 + 7
FT = 15
MT = 15
H1 = 1852
N2 = 256
EPS = 1e-5
V_ITEM, V_CITY, V_CP, V_PRICE, V_IMP, V_ACT = 62500, 6250, 7500, 30, 30, 10
SMALL = T + 4
G_ITEM, G_LAST, G_LCI, G_CITY, G_CP, G_POOL = range(6)
(X_PRICE, X_IMP, X_LCIMP, X_LII, X_ITEM, X_POOL, X_CITY, X_LAST, X_LCI, X_CP, X_INTER, X_ILAST, X_ILC, X_IMPL,
 X_SESS) = range(FT)
REFERENCE_TILES = (X_ITEM, X_POOL, X_PRICE, X_CITY, X_LAST, X_IMP, X_INTER, X_ILAST, X_SESS, X_LCI, X_LCIMP,
                   X_LII, X_ILC, X_IMPL, X_CP)
NS = 4
FD = FT - NS
NG = FT - 1
EARLY = 8
ROWS = 96
V_SMALL = 30
R_SECOND, R_CONT, R_CONT2, R_SUM2, R_NEIGH, R_SQ = 0, 1, 32, 64, 65, 96
N_CONT, N_NEIGH = 20, 25


def rec_kernel(nc, d, out):
    xT_dram = nc.dram_tensor("session_x_T", (T, P, B), F32, kind="Internal").ap()
    h0_dram = nc.dram_tensor("layer0_h_T", (T, P, B), F32, kind="Internal").ap()
    small_dram = nc.dram_tensor("small_ids", (SMALL, B), BF16, kind="Internal").ap()

    ctx = ExitStack()
    with ctx:
        def sb(name, shape, dt=F32):
            return ctx.enter_context(nc.sbuf_tensor(name, shape, dt))

        def sem(name):
            return ctx.enter_context(nc.semaphore(name))

        ident = sb("ident", [P, P])
        ones = sb("ones", [P, 1])
        cmp_act = sb("cmp_act", [2 * 32, 1])
        cmp_emb = sb("cmp_emb", [ROWS, 1])
        small_lim = sb("small_lim", [SMALL, 2])
        wx = [sb(f"wx{l}", [P, 2, 3, H]) for l in range(2)]
        wa = sb("wa", [P, 2, 3, H])
        wh = [sb(f"wh{l}", [P, 3, 2 * H]) for l in range(2)]
        bih = sb("bih", [P, 2, 3])
        bhh = sb("bhh", [P, 2, 3])
        brz = sb("brz", [P, 2, 3])
        brz_neg = sb("brz_neg", [P, 2, 3])
        act_T = sb("act_T", [P, V_ACT])
        act_tab = sb("act_tab", [64, 3, 2 * H], BF16)
        emb_s = sb("emb_s", [V_SMALL, 2, P])
        emb_tab = sb("emb_tab", [ROWS, 2, P], BF16)
        emb_T = sb("emb_T", [P, 2, V_SMALL])
        emb_n = sb("emb_n", [P, NS, V_SMALL])
        bn1 = sb("bn1", [P, 2, FT])
        bn2 = sb("bn2", [P, 2, MT + 1])
        b1 = sb("b1", [P, MT])
        b2 = sb("b2", [P, 2])
        wout = sb("wout", [P, 2])
        bout = sb("bout", [1, 1])
        prime = sb("prime", [1, 16])
        NCOL = T + NPAST + 5
        ids = sb("ids", [P, NCOL * BT], I32)
        ids_ok = sb("ids_ok", [P, NCOL * BT], I32)
        ids_now = sb("ids_now", [P, 2, 2 * BT], I32)
        other = sb("other", [P, B])
        mv1 = sb("mv1", [P, FT, 2])
        st = sb("st", [P, FT, 2, 6])
        std = sb("std", [P, FT])
        ac = sb("ac", [P, 2, FT])
        tmp = sb("tmp", [P, FT])
        st2 = sb("st2", [P, 2, 2, 6])
        mv2 = sb("mv2", [P, 2, 2])
        fold2 = sb("fold2", [P, 2, 5])
        w2r = sb("w2r", [P, 3, N2])
        w1r = sb("w1r", [P, 2, FT, P])
        with nc.sbuf_tensor("XH", [P, FT, B], F32) as XH:
            pass
        sb("XH_tables", [P, NS, B])
        x_lo = sb("x_lo", [P, FD, B], F32R)
        with ExitStack() as gru:
            def gb(name, shape, dt=F32):
                return gru.enter_context(nc.sbuf_tensor(name, shape, dt))

            h = gb("h", [P, C, CW])
            h_hi = gb("h_hi", [P, C, CW], F32R)
            h_lo = gb("h_lo", [P, C, CW], F32R)
            wh_hi = gb("wh_hi", [P, 2, 3, 2 * H], F32R)
            wh_lo = gb("wh_lo", [P, 2, 3, 2 * H], F32R)
            onehot = gb("onehot", [64, 2, B], BF16)
            act_rows = gb("act_rows", [64, 2, B], BF16)
            E = gb("E", [P, 6, BT, P])
            work = gb("work", [P, 14 * B])
        h1 = sb("h1", [P, 2, B])
        y_hi = sb("y_hi", [P, B], F32R)
        y_lo = sb("y_lo", [P, B], F32R)
        w2_hi = sb("w2_hi", [P, N2], F32R)
        w2_lo = sb("w2_lo", [P, N2], F32R)
        x_hi = sb("x_hi", [P, FD, B], F32R)
        w_hi = sb("w_hi", [P, 2, FD, P], F32R)
        w_lo = sb("w_lo", [P, 2, FD, P], F32R)
        sb("space", [P, 6 * P * 2])
        feat_oh = sb("feat_oh", [ROWS, NS, B], BF16)
        tab = sb("tab", [ROWS, 2, NS * P], BF16)
        tab_mid = sb("tab_mid", [V_SMALL, NS * P], BF16)
        tab_rest = sb("tab_rest", [V_SMALL, 2, NS * P])
        xs = work[:, 0:4 * B].rearrange("p (par f b) -> p par f b", par=2, f=2)
        xe = work[:, 4 * B:8 * B].rearrange("p (par f b) -> p par f b", par=2, f=2)
        ring = work[:, 8 * B:12 * B].rearrange("p (par f t e) -> p par f t e", par=2, f=2, t=BT)
        gate_tiles = ([XH[:, k, :] for k in (9, 10, 11, 12)], [xe[:, k // 2, k % 2, :] for k in range(4)])
        r, z, n, zc = ([tiles[k].rearrange("p (c b) -> p c b", c=C) for tiles in gate_tiles] for k in range(4))
        acc = work[:, 8 * B:10 * B].rearrange("p (k b) -> p k b", k=2)
        sq = E[:, 0].rearrange("p t e -> p (t e)")
        t_buf = work[:, 12 * B:13 * B].rearrange("p (c b) -> p c b", c=C)
        zh = work[:, 13 * B:14 * B].rearrange("p (c b) -> p c b", c=C)
        small_i = w1r[0:SMALL, 0, 0:8, :].rearrange("p a b -> p (a b)").bitcast(I32)
        small_f = XH[0:SMALL, 0, :]
        small_g = XH[0:SMALL, 1, :]
        small_b = XH[0:SMALL, 2, 0:B // 2].bitcast(BF16)
        ids_neg = XH[:, 3, 0:NCOL * BT]
        part_rest = XH[0:V_ACT, 4, 0:2 * 6 * H].rearrange("p (k n) -> p k n", k=2)
        part = XH[0:V_ACT, 5, 0:3 * 6 * H // 2].bitcast(BF16).rearrange("p (k n) -> p k n", k=3)
        emb_rest = XH[0:30, 9, 0:2 * 2 * P].rearrange("p (k e n) -> p k e n", k=2, e=2)
        emb_part = XH[0:30, 10, 0:3 * P].bitcast(BF16).rearrange("p (k e n) -> p k e n", k=3, e=2)
        feat_rows = XH[0:ROWS, 6:8, :].rearrange("p a b -> p (a b)").bitcast(BF16).rearrange("p (k b) -> p k b", k=4)
        sum2 = h1[0:1, 0, :]
        h2 = h1
        y = tab_rest[0:1].rearrange("p a b -> p (a b)")

        ps = ctx.enter_context(nc.psum_tensor("ps", [P, 8, CW], F32))
        ps_r, ps_z, ps_xn = ps[:, 0:2, :], ps[:, 2:4, :], ps[:, 4:6, :]
        ps_t = ps[:, 7, :]

        def ps_hn(c, own):
            return ps[:, 6 + c * own, :]

        s_pre_w = sem("weights_loaded")
        s_ids, s_sids = sem("ids_loaded"), sem("small_ids_loaded")
        s_idok, s_sidok = sem("ids_clamped"), sem("small_ids_clamped")
        s_small = sem("small_ids_stored")
        s_dve = sem("dve_setup")
        s_parts = sem("act_table_parts_placed")
        s_tabps = sem("act_table_product")
        s_now = sem("pair_ids_copied")
        s_gath = [sem(f"pair_gathered{i}") for i in range(2)]
        s_fgath = sem("features_gathered")
        s_fring = sem("past_column_gathered")
        s_fpool = sem("past_column_pooled")
        s_fnow = sem("past_ids_copied")
        s_t = sem("quarter_transposed")
        s_ev = sem("quarter_evacuated")
        s_xd = [sem(f"pair_x_stored{i}") for i in range(2)]
        s_xs = [sem(f"step_x_loaded{i}") for i in range(2)]
        s_ar = [sem(f"step_actions_loaded{i}") for i in range(2)]
        s_oh = sem("onehot_built")
        s_px = sem("input_products_done")
        s_pr, s_phn, s_pz = sem("r_product"), sem("hn_product"), sem("z_product")
        s_r, s_z, s_n = sem("r_gate"), sem("z_gate"), sem("n_gate")
        s_t1, s_t2, s_zh, s_zc, s_m, s_h = (sem("r_times_hn"), sem("n_argument"), sem("z_times_h"),
                                            sem("banks_free"), sem("n_part"), sem("h_new"))
        s_hs = [sem(f"h_stored{c}") for c in range(C)]
        s_hhi, s_hlo, s_wsp = sem("h_high_part"), sem("h_low_part"), sem("recurrent_weights_split")
        s_max = sem("session_max")
        s_ft, s_fe = sem("feature_product"), [sem("feature_evacuated_by_act"), sem("feature_evacuated_by_dve")]
        s_frow = sem("feature_rows_loaded")
        s_foh = sem("feature_onehots")
        s_fx = sem("feature_norm_steps")
        s_stat = sem("statistics_then_table_memory_zeroed")
        s_feat = sem("all_features_but_session")
        s_pw = sem("pool_feature_step")
        s_acc = sem("row_sums_accumulated")
        s_rows = sem("row_sums")
        s_sum = sem("sum_rows_placed")
        s_plo = sem("early_features_split")
        s_oth = sem("other_rows")
        s_c2 = sem("cont_squared")
        s_sqrt = sem("deviation")
        s_app = sem("late_feature_low_part")
        s_w1 = [sem(f"w1_loaded{i}") for i in range(2)]
        s_hi, s_lo = sem("w1_high_part"), sem("w1_low_part")
        s_xhi = sem("x_high_part")
        s_m1 = sem("dense1_product")
        s_m1e = sem("dense1_relu")
        s_nact = sem("session_feature_normalised")
        s_embn = sem("small_tables_normalised")
        s_tp = sem("table_product")
        s_tab = sem("table_parts")
        s_yhi, s_ylo = sem("second_input_high_part"), sem("second_input_and_weights_low_parts")
        s_w2hi = sem("w2_high_part")
        s_bn = sem("second_norm_step")
        s_dev = sem("second_deviation")
        s_norm = sem("tile_normalised")
        s_w2 = [sem(f"w2_loaded{i}") for i in range(3)]
        s_m2 = sem("dense2_product")
        s_m2e = sem("dense2_relu")
        s_y = sem("logit")
        s_ye = sem("output_ready")
        s_out = sem("output_stored")
        s_tick_pool, s_tick_sp = sem("tick_pool"), sem("tick_sp")
        s_tick_act, s_tick_dve = sem("tick_act"), sem("tick_dve")

        N_W = 20
        L1N = 2 * T

        def col(j):
            return ids_ok[:, j * BT:(j + 1) * BT]

        block = ctx.enter_context(nc.Block())

        @block.sync
        def _(sp):
            sp.dma_start(ids[:], d["ids"]).then_inc(s_ids, 16)
            sp.dma_start(small_i, d["small"]).then_inc(s_sids, 16)
            sp.dma_start(small_lim[:], d["small_lim"]).then_inc(s_sids, 16)
            for dst, src in ((ident[:], d["ident"]), (cmp_act[:], d["cmp_act"]), (cmp_emb[:], d["cmp_emb"]),
                             (wx[0][:], d["wih0"][0:P]), (wa[:], d["wih0"][P:2 * P]), (wx[1][:], d["wih1"]),
                             (bih[:], d["bih"]), (bhh[:], d["bhh"]), (act_T[:], d["act_T"]),
                             (emb_s[:, 0, :], d["emb_price"]), (emb_s[:, 1, :], d["emb_imp"]),
                             (emb_T[:], d["emb_T"]),
                             (bn1[:], d["bn1"]), (bn2[:], d["bn2"]), (b1[:], d["b1"]), (b2[:], d["b2"])):
                sp.dma_start(dst, src).then_inc(s_pre_w, 16)
            sp.wait_ge(s_dve, 1)
            for l in range(2):
                for f in range(2):
                    sp.dma_start(wh[l][f * H:(f + 1) * H, :, f * H:(f + 1) * H], d[f"whh{l}"][f]).then_inc(s_pre_w, 16)
            sp.wait_ge(s_sidok, 3)
            sp.dma_start(small_dram, small_b).then_inc(s_small, 16)
            sp.wait_ge(s_tabps, 2)
            for k in range(3):
                for f in range(2):
                    sp.dma_start(act_tab[32 * f + 10 * k:32 * f + 10 * k + 10, :, f * H:(f + 1) * H],
                                 part[:, k, :].rearrange("p (f g n) -> p f g n", f=2, g=3)[:, f]).then_inc(s_parts, 16)
                sp.dma_start(emb_tab[32 * k:32 * k + V_SMALL, :, :], emb_part[:, k, :, :]).then_inc(s_parts, 16)

            def load_x(S, par):
                sp.dma_start(xs[:, par, 0, :], xT_dram[S]).then_inc(s_xs[par], 16)
                sp.dma_start(xs[:, par, 1, :], xT_dram[T - 1 - S]).then_inc(s_xs[par], 16)

            def load_actions(S, par):
                sp.dma_start(act_rows[0:32, par, :], small_dram[S].partition_broadcast(32)).then_inc(s_ar[par], 16)
                sp.dma_start(act_rows[32:64, par, :], small_dram[T - 1 - S].partition_broadcast(32))\
                    .then_inc(s_ar[par], 16)

            def load1(S, par):
                sp.dma_start(xs[:, par, 0, :], h0_dram[S]).then_inc(s_xs[par], 16)
                sp.dma_start(xs[:, par, 1, :], h0_dram[T - 1 - S]).then_inc(s_xs[par], 16)

            def store_h(S):
                for c in range(C):
                    sp.wait_ge(s_h, 2 * S + c + 3)
                    sp.dma_start(h0_dram[S, 0:H, c * CW:(c + 1) * CW], h[0:H, c, :]).then_inc(s_hs[c], 16)
                    sp.dma_start(h0_dram[T - 1 - S, H:P, c * CW:(c + 1) * CW], h[H:P, c, :]).then_inc(s_hs[c], 16)

            sp.wait_ge(s_small, 16)
            load_actions(0, 0)
            load_actions(1, 1)
            for k in range(NS):
                sp.dma_start(feat_rows[:, k, :], small_dram[T + k].partition_broadcast(ROWS)).then_inc(s_frow, 16)
            sp.wait_ge(s_c2, 1)
            sp.dma_start(other[R_CONT:R_CONT + N_CONT, :], d["cont_T"]).then_inc(s_oth, 16)
            sp.dma_start(other[R_CONT2:R_CONT2 + N_CONT, :], d["cont_T"]).then_inc(s_oth, 16)
            sp.dma_start(other[R_NEIGH:R_NEIGH + N_NEIGH, :], d["neigh_T"]).then_inc(s_oth, 16)
            sp.dma_start(wout[:], d["wout"]).then_inc(s_oth, 16)
            sp.dma_start(bout[:], d["bout"]).then_inc(s_oth, 16)
            sp.dma_start(w2r[:, 2], d["w2"][:, MT]).then_inc(s_w2[2], 16)
            with sp.Fori(0, OWN // 2) as i:
                for u in range(2):
                    S = i * 2 + u
                    sp.wait_ge(s_oh, S + 1)
                    load_actions(S + 2, u)
                    store_h(S)
            sp.wait_ge(s_xd[0], 32 * 8 + 1)
            sp.wait_ge(s_xd[1], 32 * 7 + 1)
            load_x(FROM_DRAM, 0)
            for S in range(OWN, FROM_DRAM):
                sp.wait_ge(s_oh, S + 1)
                load_actions(S + 2, S % 2)
                if S < FROM_DRAM - 1:
                    store_h(S)
            with sp.Fori(FROM_DRAM // 2, T // 2 - 1) as i:
                for u in range(2):
                    S = i * 2 + u
                    sp.wait_ge(s_px, S * 2 + 2)
                    sp.sem_inc(s_tick_sp, 1)
                    load_x(S + 1, (u + 1) % 2)
                    sp.wait_ge(s_oh, S + 1)
                    load_actions(S + 2, u)
                    store_h(S - 1)
            sp.wait_ge(s_px, 2 * (T - 2) + 2)
            load_x(T - 1, 1)
            for S in range(T - 3, T):
                store_h(S)
            for c in range(C):
                sp.wait_ge(s_hs[c], 32 * T + 1)
            load1(0, 0)
            with sp.Fori(0, T // 2 - 1) as i:
                for u in range(2):
                    S = i * 2 + u
                    sp.wait_ge(s_px, S * 2 + 2 + L1N)
                    load1(S + 1, (u + 1) % 2)
            sp.wait_ge(s_px, 2 * (T - 2) + 2 + L1N)
            load1(T - 1, 1)
            for m in range(2):
                sp.dma_start(w1r[:, m], d["w1"][m]).then_inc(s_w1[m], 16)
                sp.dma_start(w2r[:, m], d["w2"][:, m]).then_inc(s_w2[m], 16)
            with sp.Fori(0, MT // 2) as i:
                for u in range(2):
                    m = i * 2 + u
                    sp.wait_ge(s_lo, m + 1)
                    sp.sem_inc(s_tick_sp, 1)
                    sp.wait_ge(s_tp, m + 1)
                    sp.dma_start(w1r[:, u], d["w1"][m + 2]).then_inc(s_w1[u], 16)
                    sp.wait_ge(s_ylo, m + 3)
                    sp.dma_start(w2r[:, u], d["w2"][:, m + 2]).then_inc(s_w2[u], 16)
            sp.wait_ge(s_w2[1], 16 * (MT // 2 + 1))
            sp.wait_ge(s_ye, 1)
            sp.dma_start(out, y).then_inc(s_out, 16)
            sp.wait_ge(s_out, 16)

        @block.gpsimd
        def _(pool):
            pool.wait_ge(s_idok, 3)

            def gather(dst, idx, table, done):
                pool.indirect_dma_start(dst, None, table,
                                        bass.IndirectOffsetOnAxis(ap=idx.bitcast(U32), axis=0)).then_inc(done, 16)

            def gather_pair(j, par, first=False):
                nc.gpsimd.tensor_copy(ids_now[:, par, :], ids_ok[:, bass.ds(j * (2 * BT), 2 * BT)]).then_inc(s_now, 1)
                pool.wait_ge(s_now, j + 1)
                pool.sem_inc(s_tick_pool, 1)
                for f in range(2):
                    for b in range(BT):
                        gather(ring[:, par, f, b, :], ids_now[:, par, f * BT + b:f * BT + b + 1], d["emb_item"],
                               s_gath[par])

            gather_pair(0, 0)
            gather_pair(1, 1)
            with pool.Fori(1, PAIRS // 2) as i:
                for u in range(2):
                    j = i * 2 + u
                    pool.wait_ge(s_t, (j - 1) * 4)
                    gather_pair(j, u)
            pool.wait_ge(s_t, (PAIRS - 2) * 4)
            gather_pair(PAIRS - 1, 0)
            for b in range(BT):
                gather(E[:, G_POOL, b, :], col(T)[:, b:b + 1], d["emb_item"], s_fring)
            pool.wait_ge(s_t, PAIRS * 4)

            def past_column(k):
                pool.wait_ge(s_fpool, k)
                nc.gpsimd.tensor_copy(ids_now[:, 1, 0:BT], ids_ok[:, bass.ds((k + T) * BT, BT)]).then_inc(s_fnow, 1)
                pool.wait_ge(s_fnow, k)
                pool.sem_inc(s_tick_pool, 1)
                for b in range(BT):
                    gather(ring[:, 0, 0, b, :], ids_now[:, 1, b:b + 1], d["emb_item"], s_fring)

            at = T + NPAST
            for k, (slot, table) in enumerate(((G_ITEM, "emb_item"), (G_LAST, "emb_item"), (G_LCI, "emb_item"),
                                               (G_CITY, "emb_city"), (G_CP, "emb_cp"))):
                past_column(k + 1)
                for b in range(BT):
                    gather(E[:, slot, b, :], col(at + slot)[:, b:b + 1], d[table], s_fgath)
            with pool.Fori(6, NPAST) as k:
                past_column(k)

            G = nc.gpsimd
            steps = [0]

            def link(ins):
                ins.then_inc(s_pw, 1)
                steps[0] += 1
                pool.wait_ge(s_pw, steps[0])

            pool.wait_ge(s_fe[0], 5)
            pool.wait_ge(s_fe[1], 5)
            for o, a, b in ((X_INTER, X_ITEM, X_POOL), (X_ILAST, X_ITEM, X_LAST), (X_ILC, X_ITEM, X_LCI),
                            (X_IMPL, X_IMP, X_LII)):
                last = G.tensor_tensor(XH[:, o, :], XH[:, a, :], XH[:, b, :], ALU.mult)
            last.then_inc(s_feat, 1)
            x0, x1 = REFERENCE_TILES[0:2]
            link(G.tensor_tensor(acc[:, 0, :], XH[:, x0, :], XH[:, x1, :], ALU.add))
            link(G.tensor_tensor(acc[:, 1, :], XH[:, x0, :], XH[:, x0, :], ALU.mult))
            link(G.tensor_tensor(sq, XH[:, x1, :], XH[:, x1, :], ALU.mult))
            for x in REFERENCE_TILES[2:6]:
                link(G.tensor_tensor(acc[:, 1, :], acc[:, 1, :], sq, ALU.add))
                link(G.tensor_tensor(acc[:, 0, :], acc[:, 0, :], XH[:, x, :], ALU.add))
                link(G.tensor_tensor(sq, XH[:, x, :], XH[:, x, :], ALU.mult))
            G.tensor_tensor(acc[:, 1, :], acc[:, 1, :], sq, ALU.add).then_inc(s_acc, 1)
            pool.wait_ge(s_fx, 6)
            for t, table in enumerate((0, 1, 1, 1)):
                last = G.tensor_scalar(emb_n[:, t, :], emb_T[:, table, :], ac[:, 0, t:t + 1], std[:, t:t + 1],
                                       ALU.mult, ALU.add)
            last.then_inc(s_embn, 1)
            for k in range(FD - 1):
                x = XH[:, NS + k, :]
                link(G.tensor_scalar(x, x, ac[:, 0, NS + k:NS + k + 1], std[:, NS + k:NS + k + 1], ALU.mult, ALU.add))
                if k < EARLY:
                    link(G.tensor_copy(x_hi[:, k, :], x))
                    G.tensor_tensor(x_lo[:, k, :], x, x_hi[:, k, :], ALU.subtract).then_inc(s_plo, 1)
            pool.sem_inc(s_plo, 1)

        @block.tensor
        def _(pe):
            pe.wait_ge(s_pre_w, 16 * N_W)
            pe.wait_ge(s_dve, 5)
            nc.tensor.matmul(ps_hn(0, 0)[0:V_ACT, 0:384], act_T[:], wa[:].rearrange("p f g n -> p (f g n)"),
                             start=True, stop=True).then_inc(s_tabps, 1)

            def transpose_quarter(q, par, w_gath, w_ev):
                if q == 0:
                    pe.wait_ge(s_gath[par], w_gath)
                pe.wait_ge(s_ev, w_ev)
                half, f = q // 2, q % 2
                for k in range(4):
                    last = nc.tensor.transpose(ps_t[:, k * P:(k + 1) * P], ring[:, par, f, 4 * half + k, :], ident[:])
                last.then_inc(s_t, 1)

            def x_product(l, c, par, N, src, swap=0):
                pe.wait_ge(s_zc, N + 1)
                for g, bank in enumerate((ps_r, ps_z, ps_xn)):
                    if g == 2:
                        pe.wait_ge(s_t2, N + 1)
                    for f in range(2):
                        last = nc.tensor.matmul(bank[f * H:(f + 1) * H, c, :], wx[l][:, f, g, :],
                                                src[:, par, f ^ swap, c * CW:(c + 1) * CW], start=True,
                                                stop=(l == 1 and g == 2), skip_group_check=True)
                if l == 0:
                    for g, bank in enumerate((ps_r, ps_z, ps_xn)):
                        last = nc.tensor.matmul(bank[:, c, :], act_tab[:, g, :],
                                                onehot[:, par ^ swap, c * CW:(c + 1) * CW], start=False, stop=(g == 2),
                                                skip_group_check=True)
                last.then_inc(s_px, 1)

            def h_product(l, c, N, own):
                def part(w, rhs, g, bank, start=False, stop=False):
                    return nc.tensor.matmul(bank, w[:, l, g, :], rhs[:, c, :], start=start, stop=stop,
                                            skip_group_check=True)

                pe.wait_ge(s_hhi, N + 1 + 2 * l)
                for w in (wh_lo, wh_hi):
                    part(w, h_hi, 0, ps_r[:, c, :])
                if not own:
                    pe.wait_ge(s_t1, N + 1)
                part(wh_lo, h_hi, 2, ps_hn(c, own), start=True)
                part(wh_hi, h_hi, 2, ps_hn(c, own))
                pe.wait_ge(s_hlo, N + 1 + 2 * l)
                part(wh_hi, h_lo, 0, ps_r[:, c, :], stop=True).then_inc(s_pr, 1)
                part(wh_hi, h_lo, 2, ps_hn(c, own), stop=True).then_inc(s_phn, 1)
                for w in (wh_lo, wh_hi):
                    part(w, h_hi, 1, ps_z[:, c, :])
                part(wh_hi, h_lo, 1, ps_z[:, c, :], stop=True).then_inc(s_pz, 1)

            for q in range(4):
                transpose_quarter(q, 0, 256, q + 1)
            pe.wait_ge(s_parts, 16 * 9)
            pe.wait_ge(s_wsp, 2)
            with pe.Fori(0, OWN // 2) as i:
                for u in range(2):
                    S = i * 2 + u
                    w_gath = (i + (u + 1) // 2 + 1) * 256
                    pe.wait_ge(s_oh, S + 1)
                    for c in range(C):
                        pe.wait_ge(s_ev, S * 4 + 2 * c + 3)
                        x_product(0, c, u, S * 2 + c, xe)
                        if c == 1:
                            transpose_quarter(1, 1 - u, w_gath, S * 4 + 6)
                        h_product(0, c, S * 2 + c, 0)
                        transpose_quarter(2 * c, 1 - u, w_gath, S * 4 + 2 * c + 5)
                    transpose_quarter(3, 1 - u, w_gath, S * 4 + 8)
            pe.wait_ge(s_ev, 4 * PAIRS + 1)
            pe.wait_ge(s_t1, 2 * OWN + 1)
            for S in range(OWN, FROM_DRAM):
                pe.wait_ge(s_oh, S + 1)
                for c in range(C):
                    x_product(0, c, 0, S * 2 + c, xe, S - OWN)
                    h_product(0, c, S * 2 + c, 1)
            with pe.Fori(FROM_DRAM // 2, T // 2) as i:
                for u in range(2):
                    S = i * 2 + u
                    pe.wait_ge(s_xs[u], (i - (FROM_DRAM // 2 - 1)) * 32)
                    pe.wait_ge(s_oh, S + 1)
                    for c in range(C):
                        x_product(0, c, u, S * 2 + c, xs)
                        h_product(0, c, S * 2 + c, 1)

            pe.wait_ge(s_fgath, 16 * BT * 5)
            pe.wait_ge(s_foh, 1)
            pe.wait_ge(s_h, 2 * T + 2)
            for k, (slot, x) in enumerate(FEATURES):
                if k >= 4:
                    pe.wait_ge(s_fe[k % 2], (k - 4) // 2 + 1)
                if slot == G_POOL and k < 6:
                    pe.wait_ge(s_fpool, NPAST)
                for half in range(2):
                    bank = ps[:, 2 * (k % 4) + half, :]
                    if k < 6:
                        for q in range(4):
                            last = nc.tensor.transpose(bank[:, q * P:(q + 1) * P], E[:, slot, 4 * half + q, :],
                                                       ident[:])
                    else:
                        last = nc.tensor.matmul(bank, emb_tab[:, slot, :], feat_oh[:, k - 6, half * CW:(half + 1) * CW],
                                                start=True, stop=True)
                last.then_inc(s_ft, 1)
            for k in range(2):
                pe.wait_ge(s_fe[k], 5)

            with pe.Fori(T // 2, T) as i:
                for u in range(2):
                    S = i * 2 + u
                    pe.wait_ge(s_xs[u], (i - (FROM_DRAM // 2 - 1)) * 32)
                    for c in range(C):
                        x_product(1, c, u, S * 2 + c, xs)
                        h_product(1, c, S * 2 + c, 1)


            def table_product(par, w_w1, w_m1e, bank=None):
                bank = 4 + 2 * par if bank is None else bank
                pe.wait_ge(s_w1[par], w_w1)
                pe.wait_ge(s_m1e, w_m1e)
                for t in range(NS):
                    last = nc.tensor.matmul(ps[0:V_SMALL, bank, t * P:(t + 1) * P], emb_n[:, t, :],
                                            w1r[:, par, t, :], start=True, stop=True)
                last.then_inc(s_tp, 1)

            def feature_products(par, half, k):
                bank, cols = ps[:, 4 + 2 * par + half, :], slice(half * CW, (half + 1) * CW)
                for w, x in ((w_lo, x_hi), (w_hi, x_lo), (w_hi, x_hi)):
                    nc.tensor.matmul(bank, w[:, par, k, :], x[:, k, cols], start=(k == 0 and w is w_lo), stop=False,
                                     skip_group_check=True)

            def onehot_products(par, half):
                for t in range(NS):
                    last = nc.tensor.matmul(ps[:, 4 + 2 * par + half, :], tab[:, par, t * P:(t + 1) * P],
                                            feat_oh[:, t, half * CW:(half + 1) * CW], start=False, stop=(t == NS - 1),
                                            skip_group_check=True)
                last.then_inc(s_m1, 1)

            def dense1(m, par, w_w1, w_m1e, between=None):
                pe.wait_ge(s_lo, m + 1)
                pe.wait_ge(s_tab, 6 * m + 6)
                for half in range(2):
                    for k in range(FD):
                        feature_products(par, half, k)
                    onehot_products(par, half)
                    if half == 0:
                        table_product(1 - par, w_w1, w_m1e)
                        if between is not None:
                            between()

            def dense2(n, start=False, stop=False):
                pe.wait_ge(s_ylo, n + 1)
                for w, x in ((w2_lo, y_hi), (w2_hi, y_lo), (w2_hi, y_hi)):
                    for m2 in range(2):
                        for half in range(2):
                            last = nc.tensor.matmul(ps[:, 2 * m2 + half, :], w[:, m2 * P:(m2 + 1) * P],
                                                    x[:, half * CW:(half + 1) * CW], start=(start and w is w2_lo),
                                                    stop=(stop and w is w2_hi and x is y_hi), skip_group_check=True)
                last.then_inc(s_m2, 1)

            pe.wait_ge(s_embn, 1)
            pe.wait_ge(s_max, 2 * T + 2)
            table_product(0, 16, 2, 6)
            pe.wait_ge(s_lo, 1)
            for k in range(FD):
                if k < EARLY:
                    pe.wait_ge(s_plo, k + 1)
                else:
                    pe.wait_ge(s_app, k - EARLY + 1)
                for half in range(2):
                    feature_products(0, half, k)
                if k == 3:
                    pe.wait_ge(s_acc, 1)
                    for j in range(2):
                        for half in range(2):
                            last = nc.tensor.matmul(ps[0:1, 2 * j + half, :], ones[:],
                                                    acc[:, j, half * CW:(half + 1) * CW], start=True, stop=True)
                    last.then_inc(s_rows, 1)
                if k == 5:
                    pe.wait_ge(s_tab, 6)
                    table_product(1, 16, 2)
            for half in range(2):
                onehot_products(0, half)
            dense1(1, 1, 32, 4, between=lambda: dense2(1, start=True))
            with pe.Fori(0, MT // 2 - 1) as i:
                for u in range(2):
                    m = i * 2 + u
                    dense2(m + 2)
                    dense1(m + 2, u, (i + (u + 3) // 2 + 1) * 16, m * 2 + 6)
            dense2(MT - 1)
            dense1(MT - 1, 0, (MT // 2 + 1) * 16, 2 * MT)
            dense2(MT)
            dense2(MT + 1, stop=True)
            pe.wait_ge(s_m2e, 4)
            for half in range(2):
                for m in range(2):
                    last = nc.tensor.matmul(ps[0:1, 4 + half, :], wout[:, m:m + 1], h2[:, m, half * CW:(half + 1) * CW],
                                            start=(m == 0), stop=(m == 1))
            last.then_inc(s_y, 1)

        @block.scalar
        def _(act):
            act.wait_ge(s_pre_w, 16 * N_W)
            act.wait_ge(s_dve, 5)

            def evacuate(j, q, par):
                act.wait_ge(s_t, j * 4 + q + 1)
                nc.scalar.activation(xe[:, par, q % 2, (q // 2) * CW:(q // 2 + 1) * CW], ps_t, ACT.Copy)\
                    .then_inc(s_ev, 1)

            def store_pair(j, par):
                act.wait_ge(s_ev, j * 4 + 5)
                act.dma_start(xT_dram[j], xe[:, par, 0, :]).then_inc(s_xd[par], 16)
                act.dma_start(xT_dram[T - 1 - j], xe[:, par, 1, :]).then_inc(s_xd[par], 16)

            def r_gate(l, c, N):
                act.wait_ge(s_pr, N + 1)
                nc.scalar.activation(r[l][:, c, :], ps_r[:, c, :], ACT.Sigmoid, bias=brz[:, l, 0:1]).then_inc(s_r, 1)

            def z_gates(l, c, N):
                act.wait_ge(s_pz, N + 1)
                nc.scalar.activation(z[l][:, c, :], ps_z[:, c, :], ACT.Sigmoid, bias=brz[:, l, 1:2]).then_inc(s_z, 1)
                nc.scalar.activation(zc[l][:, c, :], ps_z[:, c, :], ACT.Sigmoid, bias=brz_neg[:, l, 1:2], scale=-1.0)\
                    .then_inc(s_zc, 1)

            def gates(l, c, N):
                r_gate(l, c, N)
                z_gates(l, c, N)

            def new(l, c, N):
                act.wait_ge(s_t2, N + 3)
                nc.scalar.activation(n[l][:, c, :], t_buf[:, c, :], ACT.Tanh, bias=bih[:, l, 2:3]).then_inc(s_n, 1)

            def high(l, c, N):
                act.wait_ge(s_h, N + 3 + 2 * l)
                nc.scalar.activation(h_hi[:, c, :], h[:, c, :], ACT.Copy).then_inc(s_hhi, 1)

            nc.scalar.activation(prime[:, 15:16], ones[0:1, :], ACT.Sigmoid)
            for q in range(4):
                evacuate(0, q, 0)
            store_pair(0, 0)
            act.wait_ge(s_oth, 80)
            nc.scalar.activation(other[R_CONT2:R_CONT2 + N_CONT, :], other[R_CONT2:R_CONT2 + N_CONT, :],
                                 ACT.Square).then_inc(s_c2, 1)
            with act.Fori(0, OWN // 2) as i:
                for u in range(2):
                    S = i * 2 + u
                    gates(0, 0, S * 2)
                    act.wait_ge(s_xd[1 - u], (i + (u + 1) // 2) * 32 + 1)
                    evacuate(S + 1, 0, 1 - u)
                    new(0, 0, S * 2)
                    evacuate(S + 1, 1, 1 - u)
                    high(0, 0, S * 2)
                    gates(0, 1, S * 2 + 1)
                    evacuate(S + 1, 2, 1 - u)
                    new(0, 1, S * 2 + 1)
                    evacuate(S + 1, 3, 1 - u)
                    high(0, 1, S * 2 + 1)
                    store_pair(S + 1, 1 - u)

            def turn(l, c, N, last=False):
                new(l, c, N)
                if not last:
                    r_gate(l, 1 - c, N + 1)
                if l == 0 or not last:
                    high(l, c, N)
                if not last:
                    z_gates(l, 1 - c, N + 1)

            def chain_steps(l, first, end):
                with act.Fori(first, end) as i:
                    for u in range(2):
                        for c in range(C):
                            turn(l, c, i * 4 + 2 * u + c)

            def last_steps(l, end):
                for N in range(4 * end - 4, 4 * end):
                    turn(l, N % 2, N, N == 4 * end - 1)

            gates(0, 0, 2 * OWN)
            chain_steps(0, OWN // 2, T // 2 - 1)
            last_steps(0, T // 2)
            for k in range(0, 10, 2):
                act.wait_ge(s_ft, k + 1)
                bk = 2 * (k % 4)
                nc.scalar.activation(XH[:, FEATURES[k][1], :], ps[:, bk:bk + 2, :].rearrange("p a b -> p (a b)"),
                                     ACT.Copy).then_inc(s_fe[0], 1)
            act.wait_ge(s_xd[0], 32 * 8 + 1)
            act.wait_ge(s_xd[1], 32 * 7 + 1)
            gates(1, 0, 2 * T)
            chain_steps(1, T // 2, STATS_END)
            act.wait_ge(s_fx, 2)
            nc.scalar.activation(tmp[:, 0:NG], tmp[:, 0:NG], ACT.Sqrt).then_inc(s_sqrt, 1)
            nc.scalar.activation(prime[:, 15:16], ones[0:1, :], ACT.Sigmoid)
            chain_steps(1, STATS_END, T - 1)
            last_steps(1, T)
            act.wait_ge(s_h, 4 * T + 4)

            def split_hi(m, par, w_w1, w_m1):
                act.wait_ge(s_w1[par], w_w1)
                if w_m1 is not None:
                    act.wait_ge(s_m1, w_m1)
                nc.scalar.activation(w_hi[:, par], w1r[:, par, NS:FT], ACT.Copy).then_inc(s_hi, 1)

            split_hi(0, 0, 16, None)
            act.wait_ge(s_plo, EARLY + 1)
            for k in range(EARLY, FD):
                if k == FD - 1:
                    act.wait_ge(s_fx, 9)
                    nc.scalar.activation(tmp[:, NG:FT], tmp[:, NG:FT], ACT.Sqrt).then_inc(s_sqrt, 1)
                    act.wait_ge(s_fx, 13)
                    nc.scalar.activation(XH[:, X_SESS, :], XH[:, X_SESS, :], ACT.Identity, bias=std[:, NG:FT],
                                         scale=ac[:, 0, NG:FT]).then_inc(s_nact, 1)
                    act.wait_ge(s_nact, 1)
                nc.scalar.activation(x_hi[:, k, :], XH[:, NS + k, :], ACT.Copy).then_inc(s_xhi, 1)
            split_hi(1, 1, 16, None)
            act.wait_ge(s_rows, 1)
            nc.scalar.activation(sum2, ps[0:1, 0:2, :].rearrange("p a b -> p (a b)"), ACT.Square).then_inc(s_sum, 1)
            nc.scalar.activation(other[R_SQ:R_SQ + 1, :], ps[0:1, 2:4, :].rearrange("p a b -> p (a b)"), ACT.Copy)\
                .then_inc(s_sum, 1)

            def deviation(par, w_bn):
                act.wait_ge(s_bn, w_bn)
                nc.scalar.activation(fold2[:, par, 0:1], fold2[:, par, 0:1], ACT.Sqrt).then_inc(s_dev, 1)

            def second_high(n, src):
                act.wait_ge(s_norm, n)
                act.sem_inc(s_tick_act, 1)
                if not isinstance(n, int) or n > 1:
                    act.wait_ge(s_m2, n - 1)
                nc.scalar.activation(y_hi[:], src, ACT.Copy).then_inc(s_yhi, 1)

            def relu1(m, par):
                act.wait_ge(s_ylo, m + 1)
                for half in range(2):
                    act.wait_ge(s_m1, m * 2 + half + 1)
                    act.sem_inc(s_tick_act, 1)
                    nc.scalar.activation(h1[:, par, half * CW:(half + 1) * CW], ps[:, 4 + 2 * par + half, :], ACT.Relu,
                                         bias=b1[:, bass.ds(m, 1)]).then_inc(s_m1e, 1)
                deviation(par, m * 7 + 10)

            deviation(0, 3)
            second_high(1, other[:])
            with act.Fori(0, MT // 2) as i:
                for u in range(2):
                    m = i * 2 + u
                    relu1(m, u)
                    split_hi(m + 2, u, (i + 2) * 16, m * 2 + 2)
                    second_high(m + 2, h1[:, u, :])
            relu1(MT - 1, 0)
            second_high(MT + 1, h1[:, 0, :])
            act.wait_ge(s_m2, MT + 1)
            for m in range(2):
                for half in range(2):
                    nc.scalar.activation(h2[:, m, half * CW:(half + 1) * CW], ps[:, 2 * m + half, :], ACT.Relu,
                                         bias=b2[:, m:m + 1]).then_inc(s_m2e, 1)
            act.wait_ge(s_y, 1)
            nc.scalar.activation(y, ps[0:1, 4:6, :].rearrange("p a b -> p (a b)"), ACT.Sigmoid, bias=bout[:])\
                .then_inc(s_ye, 1)

        @block.vector
        def _(dve):
            V = nc.vector
            for l in range(2):
                last = V.memset(wh[l][:], 0.0)
            last.then_inc(s_dve, 1)
            dve.wait_ge(s_ids, 16)
            n_item = (T + NPAST + 3) * BT
            ranges = ((0, n_item, V_ITEM), (n_item, n_item + BT, V_CITY), (n_item + BT, n_item + 2 * BT, V_CP))
            for a, b, v in ranges:
                last = V.tensor_scalar(ids_neg[:, a:b], ids[:, a:b], 0.0, float(v), ALU.is_lt, ALU.mult)
            last.then_inc(s_idok, 1)
            dve.wait_ge(s_idok, 1)
            V.tensor_tensor(ids_neg, ids[:], ids_neg, ALU.add).then_inc(s_idok, 1)
            dve.wait_ge(s_idok, 2)
            for a, b, v in ranges:
                last = V.tensor_scalar(ids_ok[:, a:b], ids_neg[:, a:b], 0.0, float(v - 1), ALU.max, ALU.min)
            last.then_inc(s_idok, 1)
            V.memset(act_tab[:], 0.0)
            V.memset(emb_tab[:], 0.0)
            V.memset(other[:], 0.0).then_inc(s_c2, 1)
            V.memset(ones[:], 1.0)
            V.memset(h[:], 0.0).then_inc(s_h, 2)
            V.memset(h_hi[:].bitcast(F32), 0.0).then_inc(s_hhi, 2)
            V.memset(h_lo[:].bitcast(F32), 0.0).then_inc(s_hlo, 2)
            V.memset(prime[:, 0:1], 0.0).then_inc(s_t2, 2)
            V.memset(prime[:, 12:13], 0.0).then_inc(s_zc, 2)
            V.memset(prime[:, 1:2], 0.0).then_inc(s_t1, 1)
            V.memset(prime[:, 2:3], 0.0).then_inc(s_ev, 1)
            for c in range(C):
                V.memset(prime[:, 6 + c:7 + c], 0.0).then_inc(s_hs[c], 1)
                V.memset(prime[:, 10 + c:11 + c], 0.0).then_inc(s_m1e, 1)
                V.memset(prime[:, 8 + c:9 + c], 0.0).then_inc(s_xd[c], 1)
            V.memset(prime[:, 5:6], 0.0).then_inc(s_fpool, 1)
            V.memset(prime[:, 3:4], 0.0).then_inc(s_px, 2)
            V.memset(prime[:, 13:14], 0.0).then_inc(s_ylo, 1)
            V.memset(XH[:, X_SESS, :], -3.0e38).then_inc(s_max, 2)
            dve.wait_ge(s_sids, 32)
            V.tensor_scalar(small_f, small_i, 0.0, small_lim[:, 0:1], ALU.is_lt, ALU.mult).then_inc(s_sidok, 1)
            dve.wait_ge(s_sidok, 1)
            V.tensor_tensor(small_g, small_i, small_f, ALU.add).then_inc(s_sidok, 1)
            dve.wait_ge(s_sidok, 2)
            V.tensor_scalar(small_b, small_g, 0.0, small_lim[:, 1:2], ALU.max, ALU.min).then_inc(s_sidok, 1)
            dve.wait_ge(s_pre_w, 16 * N_W)
            for l in range(2):
                last = V.tensor_copy(wh_hi[:, l], wh[l][:])
            last.then_inc(s_wsp, 1)
            dve.wait_ge(s_wsp, 1)
            for l in range(2):
                last = V.tensor_tensor(wh_lo[:, l], wh[l][:], wh_hi[:, l], ALU.subtract)
            last.then_inc(s_wsp, 1)
            V.tensor_tensor(brz[:], bih[:], bhh[:], ALU.add).then_inc(s_dve, 2)
            dve.wait_ge(s_dve, 3)
            V.tensor_scalar(brz_neg[:], brz[:], -1.0, None, ALU.mult).then_inc(s_dve, 2)
            dve.wait_ge(s_tabps, 1)
            count = [5]

            def link(ins):
                ins.then_inc(s_dve, 1)
                count[0] += 1
                dve.wait_ge(s_dve, count[0])

            for parts, rest, src in ((part, part_rest, ps_hn(0, 0)[0:V_ACT, 0:384]), (emb_part, emb_rest, emb_s[:])):
                link(V.tensor_copy(parts[:, 0], src))
                link(V.tensor_tensor(rest[:, 0], src, parts[:, 0], ALU.subtract))
                link(V.tensor_copy(parts[:, 1], rest[:, 0]))
                link(V.tensor_tensor(rest[:, 1], rest[:, 0], parts[:, 1], ALU.subtract))
                link(V.tensor_copy(parts[:, 2], rest[:, 1]))
            V.memset(prime[:, 4:5], 0.0).then_inc(s_tabps, 1)

            def build_onehot(S, par, w_rows):
                dve.wait_ge(s_ar[par], w_rows)
                dve.wait_ge(s_px, S * 2)
                V.tensor_scalar(onehot[:, par, :], act_rows[:, par, :], cmp_act[:], None, ALU.is_equal)\
                    .then_inc(s_oh, 1)

            def head(l, c, N, own=1):
                dve.wait_ge(s_r, N + 1)
                dve.wait_ge(s_phn, N + 1)
                V.scalar_tensor_tensor(t_buf[:, c, :], ps_hn(c, own), bhh[:, l, 2:3], r[l][:, c, :], ALU.add, ALU.mult)\
                    .then_inc(s_t1, 1)

            def cell(l, c, N, w_store, extra=None):
                dve.wait_ge(s_t1, N + 2)
                V.tensor_tensor(t_buf[:, c, :], t_buf[:, c, :], ps_xn[:, c, :], ALU.add).then_inc(s_t2, 1)
                dve.wait_ge(s_z, N + 1)
                V.tensor_tensor(zh[:, c, :], z[l][:, c, :], h[:, c, :], ALU.mult).then_inc(s_zh, 1)
                if extra is not None:
                    extra()
                dve.wait_ge(s_zh, N + 1)
                dve.wait_ge(s_zc, N + 3)
                dve.wait_ge(s_n, N + 1)
                V.tensor_tensor(n[l][:, c, :], n[l][:, c, :], zc[l][:, c, :], ALU.mult).then_inc(s_m, 1)
                dve.wait_ge(s_m, N + 1)
                if w_store is not None:
                    dve.wait_ge(s_hs[c], w_store)
                V.tensor_tensor(h[:, c, :], n[l][:, c, :], zh[:, c, :], ALU.add).then_inc(s_h, 1)

            def low(l, c, N):
                dve.wait_ge(s_hhi, N + 3 + 2 * l)
                V.tensor_tensor(h_lo[:, c, :], h[:, c, :], h_hi[:, c, :], ALU.subtract).then_inc(s_hlo, 1)

            def past_max(k):
                dve.wait_ge(s_fring, (k + 1) * (16 * BT))
                dve.wait_ge(s_fpool, k)
                V.tensor_tensor(E[:, G_POOL], E[:, G_POOL], ring[:, 0, 0], ALU.max).then_inc(s_fpool, 1)

            def chain_steps0(first, end, own, with_past=False):
                with dve.Fori(first, end) as i:
                    for u in range(2):
                        S = i * 2 + u
                        cell(0, 0, S * 2, S * 32 + 1,
                             lambda: build_onehot(S + 1, (u + 1) % 2, (i + (u + 1) // 2 + 1) * 32))
                        head(0, 1, S * 2 + 1, own)
                        low(0, 0, S * 2)
                        cell(0, 1, S * 2 + 1, S * 32 + 1)
                        head(0, 0, S * 2 + 2, own)
                        low(0, 1, S * 2 + 1)
                    if with_past:
                        past_max(i - (T // 2 - NPAST + 1))

            build_onehot(0, 0, 32)
            head(0, 0, 0, 0)
            chain_steps0(0, OWN // 2, 0)
            chain_steps0(OWN // 2, T // 2 - 1, 1, with_past=True)
            dve.wait_ge(s_frow, 64)
            dve.wait_ge(s_t, 4 * PAIRS)
            V.tensor_scalar(feat_oh[:, :, :], feat_rows[:, :, :], cmp_emb[:], None, ALU.is_equal).then_inc(s_foh, 1)
            N_LAST = 2 * T - 1
            for N in range(N_LAST - 3, N_LAST + 1):
                cell(0, N % 2, N, 32 * (N // 2) + 1,
                     (lambda: build_onehot(T - 1, 1, 32 * (T // 2))) if N == N_LAST - 3 else None)
                if N < N_LAST:
                    head(0, (N + 1) % 2, N + 1)
                low(0, N % 2, N)
                if N == N_LAST - 2:
                    past_max(NPAST - 2)
            past_max(NPAST - 1)
            for k in range(1, 10, 2):
                dve.wait_ge(s_ft, k + 1)
                bk = 2 * (k % 4)
                V.tensor_copy(XH[:, FEATURES[k][1], :], ps[:, bk:bk + 2, :].rearrange("p a b -> p (a b)"))\
                    .then_inc(s_fe[1], 1)
            for c in range(C):
                dve.wait_ge(s_hs[c], 32 * T + 1)
            dve.wait_ge(s_hlo, 2 * T + 2)
            V.memset(h[:], 0.0).then_inc(s_h, 2)
            V.memset(h_hi[:].bitcast(F32), 0.0).then_inc(s_hhi, 2)
            V.memset(h_lo[:].bitcast(F32), 0.0).then_inc(s_hlo, 2)

            def cell_max(c, N, stats=None, last=False):
                cell(1, c, N, None, stats)
                if not last:
                    head(1, 1 - c, N + 1)
                    low(1, c, N)
                dve.wait_ge(s_h, N + 5)
                dve.wait_ge(s_max, N - (2 * T - 2))
                V.tensor_tensor(XH[:, X_SESS, c * CW:(c + 1) * CW], XH[:, X_SESS, c * CW:(c + 1) * CW],
                                h[:, c, :], ALU.max).then_inc(s_max, 1)

            def chain_steps1(first, end, with_stats):
                with dve.Fori(first, end) as i:
                    for u in range(2):
                        for c in range(C):
                            k = i * 2 + (u - T)

                            def stats():
                                V.bn_stats(st[:, bass.ds(k, 1), c, :], XH[:, bass.ds(k, 1), c * CW:(c + 1) * CW])

                            cell_max(c, i * 4 + 2 * u + c, stats if with_stats else None)

            head(1, 0, 2 * T)
            dve.wait_ge(s_fe[0], 5)
            chain_steps1(T // 2, T // 2 + 3, True)
            dve.wait_ge(s_feat, 1)
            chain_steps1(T // 2 + 3, STATS_END, True)
            def fold(a, b, at, w_sqrt):
                dve.wait_ge(s_fx, at)
                V.tensor_scalar(tmp[:, a:b], mv1[:, a:b, 1], EPS, None, ALU.add).then_inc(s_fx, 1)
                dve.wait_ge(s_sqrt, w_sqrt)
                V.reciprocal(std[:, a:b], tmp[:, a:b]).then_inc(s_fx, 1)
                dve.wait_ge(s_fx, at + 2)
                V.tensor_tensor(ac[:, 0, a:b], std[:, a:b], bn1[:, 0, a:b], ALU.mult).then_inc(s_fx, 1)
                dve.wait_ge(s_fx, at + 3)
                V.tensor_tensor(ac[:, 1, a:b], ac[:, 0, a:b], mv1[:, a:b, 0], ALU.mult).then_inc(s_fx, 1)
                dve.wait_ge(s_fx, at + 4)
                V.tensor_tensor(std[:, a:b], bn1[:, 1, a:b], ac[:, 1, a:b], ALU.subtract).then_inc(s_fx, 1)

            V.memset(prime[:, 14:15], 0.0).then_inc(s_stat, 1)
            dve.wait_ge(s_stat, 1)
            for k in range(NG):
                last = V.bn_aggr(mv1[:, k, :], st[:, k, :, :].rearrange("p a b -> p (a b)"))
            last.then_inc(s_fx, 1)
            fold(0, NG, 1, 1)
            chain_steps1(STATS_END, T - 1, False)
            for N in range(4 * T - 4, 4 * T):
                cell_max(N % 2, N, None, N == 4 * T - 1)
            def split_lo(m, par, w_m1):
                if w_m1 is not None:
                    dve.wait_ge(s_m1, w_m1)
                dve.wait_ge(s_hi, m + 1)
                V.tensor_tensor(w_lo[:, par], w1r[:, par, NS:FT], w_hi[:, par], ALU.subtract).then_inc(s_lo, 1)

            def normalise(par, m, src, col, at):
                for half in range(2):
                    if m is not None:
                        dve.wait_ge(s_m1e, m * 2 + half + 3)
                    last = V.bn_stats(st2[:, par, half, :], src[:, half * CW:(half + 1) * CW])
                last.then_inc(s_bn, 1)
                dve.wait_ge(s_bn, at + 1)
                dve.sem_inc(s_tick_dve, 1)
                V.bn_aggr(mv2[:, par, :], st2[:, par].rearrange("p a b -> p (a b)")).then_inc(s_bn, 1)
                dve.wait_ge(s_bn, at + 2)
                V.tensor_scalar(fold2[:, par, 0:1], mv2[:, par, 1:2], EPS, None, ALU.add).then_inc(s_bn, 1)
                dve.wait_ge(s_dev, 1 if m is None else m + 2)
                V.reciprocal(fold2[:, par, 1:2], fold2[:, par, 0:1]).then_inc(s_bn, 1)
                dve.wait_ge(s_bn, at + 4)
                V.tensor_tensor(fold2[:, par, 2:3], fold2[:, par, 1:2], bn2[:, 0, col], ALU.mult).then_inc(s_bn, 1)
                dve.wait_ge(s_bn, at + 5)
                V.tensor_tensor(fold2[:, par, 3:4], fold2[:, par, 2:3], mv2[:, par, 0:1], ALU.mult).then_inc(s_bn, 1)
                dve.wait_ge(s_bn, at + 6)
                V.tensor_tensor(fold2[:, par, 4:5], bn2[:, 1, col], fold2[:, par, 3:4], ALU.subtract).then_inc(s_bn, 1)
                dve.wait_ge(s_bn, at + 7)
                V.tensor_scalar(src, src, fold2[:, par, 2:3], fold2[:, par, 4:5], ALU.mult, ALU.add).then_inc(s_norm, 1)

            def tables(m, par, w_m1, bank=None):
                def step(k, ins):
                    ins.then_inc(s_tab, 1)
                    dve.wait_ge(s_tab, m * 6 + k)
                    dve.sem_inc(s_tick_dve, 1)

                dve.wait_ge(s_tp, m + 1)
                dve.sem_inc(s_tick_dve, 1)
                if w_m1 is not None:
                    dve.wait_ge(s_m1, w_m1)
                src = ps[0:V_SMALL, 4 + 2 * par if bank is None else bank, :]
                step(1, V.tensor_copy(tab[0:V_SMALL, par, :], src))
                step(2, V.tensor_tensor(tab_rest[:, 0, :], src, tab[0:V_SMALL, par, :], ALU.subtract))
                step(3, V.tensor_copy(tab_mid[:], tab_rest[:, 0, :]))
                V.tensor_copy(tab[32:32 + V_SMALL, par, :], tab_mid[:]).then_inc(s_tab, 1)
                step(5, V.tensor_tensor(tab_rest[:, 1, :], tab_rest[:, 0, :], tab_mid[:], ALU.subtract))
                V.tensor_copy(tab[64:64 + V_SMALL, par, :], tab_rest[:, 1, :]).then_inc(s_tab, 1)

            def second_low(n, slot, w_w2, src):
                dve.wait_ge(s_w2[slot], w_w2)
                dve.sem_inc(s_tick_dve, 1)
                if not isinstance(n, int) or n > 1:
                    dve.wait_ge(s_m2, n - 1)
                V.tensor_copy(w2_hi[:], w2r[:, slot, :]).then_inc(s_w2hi, 1)
                dve.wait_ge(s_yhi, n)
                V.tensor_tensor(y_lo[:], src, y_hi[:], ALU.subtract)
                dve.wait_ge(s_w2hi, n)
                V.tensor_tensor(w2_lo[:], w2r[:, slot, :], w2_hi[:], ALU.subtract).then_inc(s_ylo, 1)

            dve.wait_ge(s_max, 2 * T + 2)
            V.memset(tab[:], 0.0).then_inc(s_stat, 1)
            split_lo(0, 0, None)
            for half in range(2):
                last = V.bn_stats(st[:, X_SESS, half, :], XH[:, X_SESS, half * CW:(half + 1) * CW])
            last.then_inc(s_fx, 1)
            dve.wait_ge(s_fx, 7)
            V.bn_aggr(mv1[:, X_SESS, :], st[:, X_SESS].rearrange("p a b -> p (a b)")).then_inc(s_fx, 1)
            fold(NG, FT, 8, 2)
            dve.wait_ge(s_stat, 2)
            tables(0, 0, None, 6)
            for k in range(EARLY, FD):
                dve.wait_ge(s_xhi, k - EARLY + 1)
                V.tensor_tensor(x_lo[:, k, :], XH[:, NS + k, :], x_hi[:, k, :], ALU.subtract).then_inc(s_app, 1)
            dve.wait_ge(s_rows, 1)
            split_lo(1, 1, None)
            tables(1, 1, None)
            dve.wait_ge(s_sum, 2)
            V.tensor_copy(other[R_SUM2:R_SUM2 + 1, :], sum2).then_inc(s_sum, 1)
            V.tensor_tensor(other[R_SECOND:R_SECOND + 1, :], sum2, ps[0:1, 2:4, :].rearrange("p a b -> p (a b)"),
                            ALU.subtract).then_inc(s_sum, 1)
            dve.wait_ge(s_sum, 4)
            V.tensor_scalar(other[R_SECOND:R_SECOND + 1, :], other[R_SECOND:R_SECOND + 1, :], 0.5, None, ALU.mult)\
                .then_inc(s_sum, 1)
            dve.wait_ge(s_sum, 5)
            dve.wait_ge(s_c2, 2)
            normalise(0, None, other[:], slice(MT, MT + 1), 0)
            second_low(1, 2, 16, other[:])
            with dve.Fori(0, MT // 2) as i:
                for u in range(2):
                    m = i * 2 + u
                    normalise(u, m, h1[:, u, :], bass.ds(m, 1), m * 7 + 7)
                    second_low(m + 2, u, (i + 1) * 16, h1[:, u, :])
                    split_lo(m + 2, u, m * 2 + 2)
                    tables(m + 2, u, m * 2 + 2)
            normalise(0, MT - 1, h1[:, 0, :], slice(MT - 1, MT), 7 * MT)
            second_low(MT + 1, 0, 16 * (MT // 2 + 1), h1[:, 0, :])


FEATURES = ((G_ITEM, X_ITEM), (G_LAST, X_LAST), (G_LCI, X_LCI), (G_CITY, X_CITY), (G_CP, X_CP), (G_POOL, X_POOL),
            (0, X_PRICE), (1, X_IMP), (1, X_LCIMP), (1, X_LII))


def kernel(**a):
    import numpy as np
    import concourse.bacc as bacc
    from concourse import mybir
    from concourse.bass_utils import run_bass_kernel_spmd

    v = {k: np.asarray(x) for k, x in a.items()}

    def w(name):
        return v["L0_rec_" + name]

    def tiles(x):
        x = x.reshape(B, -1)
        return x.reshape(BT, P, -1).transpose(1, 2, 0)

    sess = v["r_past_interactions_sess"]
    order = [t for j in range(PAIRS) for t in (j, T - 1 - j)]
    cols = [tiles(sess[:, order]), tiles(v["r_past_interactions"])]
    cols += [tiles(v[k]) for k in ("r_item_id", "r_last_item", "r_last_click_item", "r_city", "r_city_platform")]
    ids = np.concatenate(cols, axis=1).reshape(P, -1)
    small = np.concatenate([v["r_past_actions_sess"].T] + [v[k][None, :] for k in (
        "r_price_rank", "r_impression_index", "r_last_click_impression", "r_last_interact_index")], axis=0)
    vocab = np.array([V_ACT] * T + [V_PRICE, V_IMP, V_IMP, V_IMP], np.float32)
    row = np.arange(64)

    def wih(x):
        return x.transpose(2, 0, 1).reshape(x.shape[2], 2, 3, H)

    def gates(x0, x1):
        return np.stack([x.reshape(2, 3, H).transpose(0, 2, 1).reshape(P, 3) for x in (x0, x1)], axis=1)

    def other(x, axis):
        x = np.moveaxis(x, axis, 0)
        res = np.zeros((MT * P + P,) + x.shape[1:], x.dtype)
        res[0:H1] = x[N_CONT:N_CONT + H1]
        o = MT * P
        e = N_CONT + H1
        res[o + R_CONT:o + R_CONT + N_CONT] = x[0:N_CONT]
        for k, dst in enumerate((R_SUM2, R_SQ, R_SECOND)):
            res[o + dst] = x[e + k]
        res[o + R_CONT2:o + R_CONT2 + N_CONT] = x[e + 3:e + 3 + N_CONT]
        res[o + R_NEIGH:o + R_NEIGH + N_NEIGH] = x[e + 3 + N_CONT:]
        return res

    in_memory = [REFERENCE_TILES.index(k) for k in range(FT)]
    w1 = np.zeros(((MT + 1) * P, FT * P), np.float32)
    w1[0:H1] = w("w1")
    b1 = np.zeros((MT * P,), np.float32)
    b1[0:H1] = w("b1")
    arrays = {
        "ids": ids,
        "small": small,
        "small_lim": np.stack([vocab, vocab - 1], axis=1),
        "ident": np.eye(P, dtype=np.float32),
        "cmp_act": np.where(row % 32 < 30, row % 32 % 10, -1).astype(np.float32)[:, None],
        "cmp_emb": np.where(np.arange(ROWS) % 32 < V_SMALL, np.arange(ROWS) % 32, -1).astype(np.float32)[:, None],
        "wih0": wih(w("gru_wih0")),
        "wih1": wih(w("gru_wih1")),
        "whh0": wih(w("gru_whh0")).transpose(1, 0, 2, 3),
        "whh1": wih(w("gru_whh1")).transpose(1, 0, 2, 3),
        "bih": gates(w("gru_bih0"), w("gru_bih1")),
        "bhh": gates(w("gru_bhh0"), w("gru_bhh1")),
        "act_T": w("emb_act").T,
        "emb_price": w("emb_price"),
        "emb_imp": w("emb_imp"),
        "emb_T": np.stack([w("emb_price").T, w("emb_imp").T], axis=1),
        "emb_item": w("emb_item"),
        "emb_city": w("emb_city"),
        "emb_cp": w("emb_cp"),
        "bn1": np.stack([w("bn_g"), w("bn_b")]).reshape(2, FT, P)[:, in_memory].transpose(2, 0, 1),
        "bn2": np.stack([other(w("bn_g"), 0), other(w("bn_b"), 0)]).reshape(2, MT + 1, P).transpose(2, 0, 1),
        "w1": w1.reshape(MT + 1, P, FT, P)[:, :, in_memory].transpose(0, 3, 2, 1),
        "b1": b1.reshape(MT, P).T,
        "w2": other(w("w2"), 1).reshape(MT + 1, P, N2).transpose(1, 0, 2),
        "b2": w("b2").reshape(2, P).T,
        "wout": w("wout").reshape(2, P).T,
        "bout": w("bout").reshape(1, 1),
        "cont_T": v["r_cont_features"].T,
        "neigh_T": v["r_neighbor_prices"].T,
    }
    arrays = {k: np.ascontiguousarray(x) for k, x in arrays.items()}
    nc = bacc.Bacc("TRN2", target_bir_lowering=False, num_devices=1)
    aps = {k: nc.dram_tensor("in_" + k, x.shape, mybir.dt.from_np(x.dtype), kind="ExternalInput").ap()
           for k, x in arrays.items()}
    out = nc.dram_tensor("out", (1, B), F32, kind="ExternalOutput").ap()
    rec_kernel(nc, aps, out)
    res = run_bass_kernel_spmd(nc, [{"in_" + k: x for k, x in arrays.items()}], core_ids=[0])
    return res.results[0]["out"].reshape(B)
```
